# Optimizing a Trainium2 kernel written in Bass

```python
import numpy as np
import jax
import jax.numpy as jnp

def _softmax(x, axis=-1):
    return jax.nn.softmax(x, axis=axis)

def _gelu(x):
    return jax.nn.gelu(x, approximate=True)

def _silu(x):
    return jax.nn.silu(x)

def _sigmoid(x):
    return jax.nn.sigmoid(x)

def _layernorm(x, axis=-1, eps=1e-05):
    m = jnp.mean(x, axis=axis, keepdims=True)
    v = jnp.var(x, axis=axis, keepdims=True)
    return (x - m) / jnp.sqrt(v + eps)

def _scatter_add(tgt, idx, src, axis=0):
    return tgt.at[idx].add(src)

def _segment_sum(src, seg, n):
    return jax.ops.segment_sum(src, seg, n)
kernel_name = 'mk_xattn_ffn_d1_seqx_r8_2e0500'

def setup_inputs(seed: int=0):
    np.random.seed(seed)
    _w = jnp.asarray

    def _rec_inputs():
        import jax
        import jax.numpy as jnp
        _rk = jax.random.key(seed)
        x = 7.22e-05 + 1 * jax.random.normal(jax.random.fold_in(_rk, 1), (16, 128, 128), jnp.float32)
        _lenS = 128 - jax.random.randint(jax.random.fold_in(_rk, 7), (16,), 0, max(1, 128 // 4) + 1, jnp.int32)
        _lenS2 = 77 - jax.random.randint(jax.random.fold_in(_rk, 8), (16,), 0, max(1, 77 // 4) + 1, jnp.int32)
        _ctx_1024P = jax.random.normal(jax.random.fold_in(_rk, 11), (16, 16, 128), jnp.float32)
        _ctx_1024c = jax.random.dirichlet(jax.random.fold_in(_rk, 511), 0.3 * jnp.ones((16,), jnp.float32), (16, 77))
        _ctx_1024t = jnp.einsum('bsk,bkd->bsd', _ctx_1024c, _ctx_1024P)
        _ctx_1024t = _ctx_1024t * jax.lax.rsqrt(jnp.mean(jnp.square(_ctx_1024t)) + 1e-12) * 0.953939
        ctx_1024 = 4.13588e-05 + 0.999923 * (_ctx_1024t + 0.3 * jax.random.normal(jax.random.fold_in(_rk, 611), (16, 77, 128), jnp.float32))
        return (x, ctx_1024)
    x, ctx_1024 = _rec_inputs()

    def _L0_xattn_setup():
        import jax, jax.numpy as jnp
        import numpy as np
        D_MODEL = 128
        NUM_HEADS = 16

        def _split(x, h):
            B, S, D = x.shape
            return x.reshape(B, S, h, D // h).transpose(0, 2, 1, 3)
        key = jax.random.key(seed)
        ks = jax.random.split(key, 12)
        B, S, D = (4, 256, D_MODEL)
        s = 1.0 / np.sqrt(D)
        inp = {'q': jax.random.normal(ks[0], (B, S, D), jnp.float32), 'k': jax.random.normal(ks[1], (B, S, D), jnp.float32), 'v': jax.random.normal(ks[2], (B, S, D), jnp.float32), 'wq': jax.random.normal(ks[3], (D, D), jnp.float32) * s, 'bq': jnp.zeros((D,), jnp.float32), 'wk': jax.random.normal(ks[4], (D, D), jnp.float32) * s, 'bk': jnp.zeros((D,), jnp.float32), 'wv': jax.random.normal(ks[5], (D, D), jnp.float32) * s, 'bv': jnp.zeros((D,), jnp.float32), 'wo': jax.random.normal(ks[6], (D, D), jnp.float32) * s, 'bo': jnp.zeros((D,), jnp.float32)}
        return inp
    _L0_xattn_all = _L0_xattn_setup()
    _L0_xattn_in = {k: v for k, v in _L0_xattn_all.items() if k in ('wq', 'bq', 'wk', 'bk', 'wv', 'bv', 'wo', 'bo')}
    del _L0_xattn_all

    def _L0_ffn_setup():
        import jax, jax.numpy as jnp
        import numpy as np
        B, S, H, F, E, R, TOPK = (4, 256, 128, 512, 4, 4, 2)

        def _more_forward(x, Wg, bg, W1, b1, W2, b2):
            b, s, h = x.shape
            cur = x
            for r in range(R):
                flat = cur.reshape(-1, h)
                logits = flat @ Wg[r] + bg[r]
                vals, idx = jax.lax.top_k(logits, TOPK)
                w = jax.nn.softmax(vals, axis=-1)
                cw = jnp.sum(jax.nn.one_hot(idx, E, dtype=flat.dtype) * w[..., None], axis=1)
                hmid = jax.nn.gelu(jnp.einsum('nh,ehf->enf', flat, W1) + b1[:, None, :])
                y = jnp.einsum('enf,efh->enh', hmid, W2) + b2[:, None, :]
                out = jnp.einsum('ne,enh->nh', cw, y)
                cur = cur + out.reshape(b, s, h)
            return cur
        key = jax.random.key(seed)
        ks = jax.random.split(key, 8)
        scale = 0.02
        return {'x': jax.random.normal(ks[0], (B, S, H), dtype=jnp.float32), 'Wg': jax.random.normal(ks[1], (R, H, E), dtype=jnp.float32) * scale, 'bg': jnp.zeros((R, E), dtype=jnp.float32), 'W1': jax.random.normal(ks[2], (E, H, F), dtype=jnp.float32) * scale, 'b1': jnp.zeros((E, F), dtype=jnp.float32), 'W2': jax.random.normal(ks[3], (E, F, H), dtype=jnp.float32) * scale, 'b2': jnp.zeros((E, H), dtype=jnp.float32)}
    _L0_ffn_all = _L0_ffn_setup()
    _L0_ffn_in = {k: v for k, v in _L0_ffn_all.items() if k in ('Wg', 'bg', 'W1', 'b1', 'W2', 'b2')}
    del _L0_ffn_all
    return {'x': x, 'ctx_1024': ctx_1024, 'L0_xattn_wq': _L0_xattn_in['wq'], 'L0_xattn_bq': _L0_xattn_in['bq'], 'L0_xattn_wk': _L0_xattn_in['wk'], 'L0_xattn_bk': _L0_xattn_in['bk'], 'L0_xattn_wv': _L0_xattn_in['wv'], 'L0_xattn_bv': _L0_xattn_in['bv'], 'L0_xattn_wo': _L0_xattn_in['wo'], 'L0_xattn_bo': _L0_xattn_in['bo'], 'L0_ffn_Wg': _L0_ffn_in['Wg'], 'L0_ffn_bg': _L0_ffn_in['bg'], 'L0_ffn_W1': _L0_ffn_in['W1'], 'L0_ffn_b1': _L0_ffn_in['b1'], 'L0_ffn_W2': _L0_ffn_in['W2'], 'L0_ffn_b2': _L0_ffn_in['b2']}

def reference(x, ctx_1024, L0_xattn_wq, L0_xattn_bq, L0_xattn_wk, L0_xattn_bk, L0_xattn_wv, L0_xattn_bv, L0_xattn_wo, L0_xattn_bo, L0_ffn_Wg, L0_ffn_bg, L0_ffn_W1, L0_ffn_b1, L0_ffn_W2, L0_ffn_b2):
    import jax
    import jax.numpy as jnp

    def _L0_xattn_ref(q, k, v, wq, bq, wk, bk, wv, bv, wo, bo):
        import jax, jax.numpy as jnp
        import numpy as np
        D_MODEL = 128
        NUM_HEADS = 16

        def _split(x, h):
            B, S, D = x.shape
            return x.reshape(B, S, h, D // h).transpose(0, 2, 1, 3)
        h = NUM_HEADS
        qp = _split(q @ wq.T + bq, h)
        kp = _split(k @ wk.T + bk, h)
        vp = _split(v @ wv.T + bv, h)
        dh = qp.shape[-1]
        scale = 1.0 / jnp.sqrt(jnp.asarray(dh, qp.dtype))
        score = jnp.einsum('bhqd,bhkd->bhqk', qp, kp) * scale
        attn = jax.nn.softmax(score, axis=-1)
        val = jnp.einsum('bhqk,bhkd->bhqd', attn, vp)
        B, _, S, _ = val.shape
        out = val.transpose(0, 2, 1, 3).reshape(B, S, h * dh)
        return out @ wo.T + bo

    def _L0_ffn_ref(x, Wg, bg, W1, b1, W2, b2):
        import jax, jax.numpy as jnp
        import numpy as np
        B, S, H, F, E, R, TOPK = (4, 256, 128, 512, 4, 4, 2)

        def _more_forward(x, Wg, bg, W1, b1, W2, b2):
            b, s, h = x.shape
            cur = x
            for r in range(R):
                flat = cur.reshape(-1, h)
                logits = flat @ Wg[r] + bg[r]
                vals, idx = jax.lax.top_k(logits, TOPK)
                w = jax.nn.softmax(vals, axis=-1)
                cw = jnp.sum(jax.nn.one_hot(idx, E, dtype=flat.dtype) * w[..., None], axis=1)
                hmid = jax.nn.gelu(jnp.einsum('nh,ehf->enf', flat, W1) + b1[:, None, :])
                y = jnp.einsum('enf,efh->enh', hmid, W2) + b2[:, None, :]
                out = jnp.einsum('ne,enh->nh', cw, y)
                cur = cur + out.reshape(b, s, h)
            return cur
        return _more_forward(x, Wg, bg, W1, b1, W2, b2)
    x = x + _L0_xattn_ref(_layernorm(x, axis=-1), ctx_1024, ctx_1024, L0_xattn_wq, L0_xattn_bq, L0_xattn_wk, L0_xattn_bk, L0_xattn_wv, L0_xattn_bv, L0_xattn_wo, L0_xattn_bo)
    x = x + _L0_ffn_ref(_layernorm(x, axis=-1), L0_ffn_Wg, L0_ffn_bg, L0_ffn_W1, L0_ffn_b1, L0_ffn_W2, L0_ffn_b2)
    return x

_drawn_inputs = setup_inputs


def setup_inputs(seed=0):
    import zlib

    import numpy as np

    out = dict(_drawn_inputs(seed))
    spreads = {'L0_xattn_bq': (0.0, 0.349),
     'L0_xattn_bk': (0.0, 0.8),
     'L0_xattn_bv': (0.0, 0.1),
     'L0_xattn_bo': (0.0, 0.1),
     'L0_ffn_bg': (0.0, 0.1),
     'L0_ffn_b1': (0.0, 0.334),
     'L0_ffn_b2': (0.0, 0.1)}
    factors = {}
    for name, (base, spread) in spreads.items():
        noise = np.random.default_rng([zlib.crc32(name.encode()), seed]).standard_normal(out[name].shape)
        drawn = base * np.exp(spread * noise) if base else spread * noise
        out[name] = jnp.asarray(drawn.astype(out[name].dtype))
    for name, factor in factors.items():
        out[name] = (out[name] * factor).astype(out[name].dtype)
    return out
```

```python
from contextlib import ExitStack

import concourse.bass as bass
from concourse import mybir

F32 = mybir.dt.float32
F32R = mybir.dt.float32r
ALU = mybir.AluOpType
ACT = mybir.ActivationFunctionType
AX_X = mybir.AxisListType.X

P = 128
EPS = 1e-5


def xattn_moe(nc, x, ctx_t, w_qkv, w_o, b_qk, b_v, b_o, wg, bg, w1, b1, w2, b2, out):
    NB, S, D = x.shape
    KEYS = ctx_t.shape[1] // NB
    KPAD = KEYS + KEYS % 2
    H, DH = 16, 8
    G, J, C = 4, 4, 4
    QUAD = 4
    QT, QK = QUAD * S, QUAD * KEYS
    NQ = NB // QUAD
    HH = H // 2
    E, R = b2.shape[1], wg.shape[1] // b2.shape[1]
    FC = b1.shape[1] // E
    T = NB * S // 2
    TG = T // P
    STEPS = E * FC
    RS = 2 * STEPS
    HALF = 512
    LAG = 3
    RING = 4
    SCALE = float(DH) ** -0.5

    with ExitStack() as stack:
        def sb(name, shape, dt=F32):
            return stack.enter_context(nc.sbuf_tensor(name, shape, dt))

        def sem(name):
            return stack.enter_context(nc.semaphore(name))

        ident = sb("ident", [P, P])
        wqkv = sb("wqkv", [P, 3, D])
        wqkv_hi = sb("wqkv_hi", [P, 3, D], F32R)
        wqkv_lo = sb("wqkv_lo", [P, 3, D], F32R)
        wo = sb("wo", [P, D])
        bqk = sb("bqk", [P, 2])
        bv = sb("bv", [KEYS, D])
        bo = sb("bo", [P, D])
        sel = sb("sel", [P, 4, G, P], F32R)
        wgs = sb("wgs", [P, R * E])
        bgs = sb("bgs", [P, R * E])
        w1_hi = sb("w1_hi", [P, STEPS * P], F32R)
        w1_lo = sb("w1_lo", [P, STEPS * P], F32R)
        w2_hi = sb("w2_hi", [P, STEPS * P], F32R)
        w2_lo = sb("w2_lo", [P, STEPS * P], F32R)
        b1s = sb("b1s", [P, STEPS])
        b2s = sb("b2s", [P, E])
        minus_half = sb("minus_half", [P, QUAD])
        later = sb("later", [P, TG, E, E])
        wins_needed = sb("wins_needed", [P, TG, E])
        xb = sb("xb", [P, NB, D])
        ctx_all = sb("ctx_all", [P, NB * KEYS])
        stats = sb("stats", [P, QUAD, 6])
        mean_var = sb("mean_var", [P, QUAD, 2])
        var_eps = sb("var_eps", [P, QUAD])
        rstd = sb("rstd", [P, QUAD])
        xn = sb("xn", [P, QUAD, D])
        ctx_hi = sb("ctx_hi", [P, QK], F32R)
        ctx_lo = sb("ctx_lo", [P, QK], F32R)
        k_full = sb("k_full", [P, QK])
        q_stack = sb("q_stack", [P, 2, G, S], F32R)
        k_stack = sb("k_stack", [P, 2, G, KPAD], F32R)
        top = sb("top", [P, 2, HH])
        sum_inv = sb("sum_inv", [P, H])
        attn_t = sb("attn_t", [P, QT])
        x1 = sb("x1", [P, NB, D])
        cur = sb("cur", [P, 2, T])
        cur_hi = sb("cur_hi", [P, 2, T], F32R)
        cur_lo = sb("cur_lo", [P, 2, T], F32R)

        hid = sb("hid", [P, 2, T])

        def parts_of(whole, *sizes):
            at = [sum(sizes[:i]) for i in range(len(sizes) + 1)]
            assert at[-1] <= whole.shape[1]
            return [whole[:, a:b] for a, b in zip(at, at[1:])]

        shared_r = sb("shared_r", [P, 2 * RING * T], F32R)
        q_hi, q_lo, k_hi, k_lo, xt_hi, xt_lo = parts_of(shared_r, NB * S, NB * S, NB * KPAD, NB * KPAD, QT, QT)
        q_hi, q_lo, k_hi, k_lo = (a.rearrange("p (b s) -> p b s", b=NB) for a in (q_hi, q_lo, k_hi, k_lo))
        hid_hi, hid_lo = (a.rearrange("p (s t) -> p s t", s=RING) for a in parts_of(shared_r, RING * T, RING * T))
        shared = sb("shared", [P, 2 * E * T])
        v_one, probs, probs_t, attn, q_full = parts_of(shared, NB * H * (DH + 1), H * KEYS, 2 * HH * S, NB * D, QT)
        v_one = v_one[0:KEYS].rearrange("p (b h d) -> p b h d", b=NB, h=H)
        probs = probs.rearrange("p (s h k) -> p s h k", s=2, h=HH)
        probs_t = probs_t[0:KEYS].rearrange("p (s h t) -> p s h t", s=2, h=HH)
        attn = attn.rearrange("p (b d) -> p b d", b=NB)
        cw_all = shared[:].rearrange("p (t e c) -> p t e c", t=2, e=E)
        w12s = sb("w12s", [P, 2 * STEPS * P])
        w1s, w2s = parts_of(w12s, STEPS * P, STEPS * P)
        cw_row = w12s[0:1, 0:E * T]
        x_or_y = sb("x_or_y", [P, NB * D])
        x_all = x_or_y[:].rearrange("p (b d) -> p b d", b=NB)
        y_w = x_or_y[:].rearrange("p (s t) -> p s t", s=2)

        ps = stack.enter_context(nc.psum_tensor("ps", [P, 8, 512], F32))
        ps_score = ps[:, 0:4]
        ps_pt = ps[0:KEYS, 4:6].rearrange("p b (h s) -> p (b h) s", s=S)
        ps_o = ps[:, 7, 0:H * (DH + 1)].rearrange("p (h d) -> p h d", d=DH + 1)
        ps_ks = ps[:, 7, 160:160 + G * KPAD].rearrange("p (g k) -> p g k", k=KPAD)

        s_in_x, s_in_w, s_in_f, s_in_w2 = sem("s_in_x"), sem("s_in_w"), sem("s_in_f"), sem("s_in_w2")
        s_ident, s_pool, s_sel, s_wsplit, s_fsplit = sem("s_ident"), sem("s_pool"), sem("s_sel"), sem("s_wsplit"), sem("s_fsplit")
        s_whi, s_unread = sem("s_whi"), sem("s_unread")
        s_stats, s_mv, s_ve, s_rstd, s_xn = sem("s_stats"), sem("s_mv"), sem("s_ve"), sem("s_rstd"), sem("s_xn")
        s_xtp, s_xth, s_xtl = sem("s_xtp"), sem("s_xth"), sem("s_xtl")
        s_qp, s_qf, s_ql = sem("s_qp"), sem("s_qf"), sem("s_ql")
        s_ctxh, s_ctx, s_kp, s_kf, s_kl = sem("s_ctxh"), sem("s_ctx"), sem("s_kp"), sem("s_kf"), sem("s_kl")
        s_vp, s_v = sem("s_vp"), sem("s_v")
        s_qsp, s_qs, s_ksp, s_ks = sem("s_qsp"), sem("s_qs"), sem("s_ksp"), sem("s_ks")
        s_score, s_top, s_sub, s_exp = sem("s_score"), sem("s_top"), sem("s_sub"), sem("s_exp")
        s_ptp, s_pt, s_pv, s_inv, s_attn = sem("s_ptp"), sem("s_pt"), sem("s_pv"), sem("s_inv"), sem("s_attn")
        s_atp, s_at, s_op, s_x1 = sem("s_atp"), sem("s_at"), sem("s_op"), sem("s_x1")
        s_ctp, s_ct, s_chi3, s_cur3 = sem("s_ctp"), sem("s_ct"), sem("s_chi3"), sem("s_cur3")
        s_w1, s_gelu, s_hi, s_lo = sem("s_w1"), sem("s_gelu"), sem("s_hi"), sem("s_lo")
        s_y, s_stt, s_acc, s_chi, s_split = sem("s_y"), sem("s_stt"), sem("s_acc"), sem("s_chi"), sem("s_split")
        s_tanh2 = sem("s_tanh2")
        s_gl, s_gate, s_arg, s_tanh, s_cw = sem("s_gl"), sem("s_gate"), sem("s_arg"), sem("s_tanh"), sem("s_cw")
        s_cwp, s_cwt, s_row, s_cwb = sem("s_cwp"), sem("s_cwt"), sem("s_row"), sem("s_cwb")
        s_ftp, s_fin, s_out = sem("s_ftp"), sem("s_fin"), sem("s_out")

        logit = sb("logit", [P, TG, E])
        hi2 = sb("hi2", [P, TG, 2])
        lo2 = sb("lo2", [P, TG, 2])
        v12 = sb("v12", [P, 4, TG])
        ge = sb("ge", [P, TG, E, E])
        beat = sb("beat", [P, TG, E, E])
        wins2 = sb("wins2", [P, TG, E, 2])
        wins = sb("wins", [P, TG, E])
        arg1 = sb("arg1", [P, TG, E])
        arg = sb("arg", [P, TG, E])
        tanh = sb("tanh", [P, TG, E])
        cw = sb("cw", [P, P])
        cw_t = sb("cw_t", [E * TG, P])
        ps_h = ps[:, 0:4].rearrange("p (s b) c -> p s (b c)", s=2)
        ps_y = ps[:, 4:6]

        block = stack.enter_context(nc.Block())

        def wait_apart(eng, semaphore, value):
            eng.wait_ge(semaphore, value)
            eng.sem_inc(s_unread, 1)

        @block.sync
        def _(sp):
            sp.dma_start(x_all, x.rearrange("b s d -> s b d")).then_inc(s_in_x, 16)
            for dst, src in ((wqkv[:], w_qkv), (ctx_all[:], ctx_t), (wo[:], w_o), (bqk[:], b_qk),
                             (bv[:], b_v[None, :].to_broadcast([KEYS, D])), (bo[:], b_o[None, :].to_broadcast([P, D]))):
                sp.dma_start(dst, src).then_inc(s_in_w, 16)
            sp.dma_start(w1s.rearrange("p (e f) -> p e f", e=E), w1.rearrange("e h f -> h e f")).then_inc(s_in_f, 16)
            for dst, src in ((wgs[:], wg), (bgs[:], bg[None, :].to_broadcast([P, R * E])), (b1s[:], b1), (b2s[:], b2)):
                sp.dma_start(dst, src).then_inc(s_in_f, 16)
            sp.dma_start(w2s.rearrange("p (c h) -> p c h", h=D), w2.rearrange("(c p) h -> p c h", p=P)).then_inc(s_in_w2, 16)

            def row(n):
                sp.wait_ge(s_cwt, n + 1)
                sp.dma_start(cw_row, cw_t[:]).then_inc(s_row, 16)

            row(0)
            with sp.Fori(0, R - 1) as r:
                row(2 * r + 1)
                row(2 * r + 2)
            row(2 * R - 1)
            for t in range(2):
                for i in range(2):
                    n = 2 * t + i
                    sp.wait_ge(s_fin, n + 1)
                    sp.dma_start(out.rearrange("b s d -> s b d")[:, 4 * n:4 * n + 4],
                                 xb[:, 4 * n:4 * n + 4]).then_inc(s_out, 16)
            sp.wait_ge(s_out, 64)

        @block.gpsimd
        def _(pool):
            nc.gpsimd.memset(ident[:], 0.0).then_inc(s_pool, 1)
            nc.gpsimd.memset(sel[:].bitcast(F32), 0.0).then_inc(s_pool, 1)
            nc.gpsimd.memset(later[:], 0.0).then_inc(s_pool, 1)
            pool.wait_ge(s_pool, 3)
            nc.gpsimd.affine_select(out=ident[:], in_=ident[:], compare_op=ALU.not_equal, fill=1.0, base=0,
                                    pattern=[[-1, P]], channel_multiplier=1).then_inc(s_ident, 1)
            nc.gpsimd.memset(v_one, 1.0).then_inc(s_pool, 1)
            nc.gpsimd.memset(k_hi.bitcast(F32), 0.0).then_inc(s_pool, 1)
            nc.gpsimd.memset(k_lo.bitcast(F32), 0.0).then_inc(s_pool, 1)
            nc.gpsimd.memset(minus_half[:], -0.5).then_inc(s_pool, 1)
            nc.gpsimd.memset(cw[:], 0.0).then_inc(s_pool, 1)
            for e in range(E):
                nc.gpsimd.memset(wins_needed[:, :, e], 2.0 - e).then_inc(s_pool, 1)
                if e < E - 1:
                    nc.gpsimd.memset(later[:, :, e, e + 1:E], 1.0).then_inc(s_pool, 1)
            pool.wait_ge(s_ident, 1)
            for kind, parts in enumerate(((0, 1), (2, 3), (0, 2), (1, 3))):
                for g in range(G):
                    for c in parts:
                        last = nc.gpsimd.tensor_copy(
                            sel[:, kind, g].rearrange("p (j c d) -> p j c d", j=J, c=C)[:, :, c],
                            ident[:].rearrange("p (j g d) -> p j g d", j=J, g=G)[:, :, g])
            last.then_inc(s_sel, 1)

            def inverse_deviation(n):
                wait_apart(pool, s_mv, n + 1)
                nc.gpsimd.tensor_scalar(var_eps[:], mean_var[:, :, 1], EPS, 1.0, ALU.add, ALU.mult).then_inc(s_ve, 1)
                pool.wait_ge(s_ve, n + 1)
                nc.gpsimd.tensor_tensor(rstd[:], var_eps[:], minus_half[:], ALU.pow).then_inc(s_rstd, 1)

            pool.wait_ge(s_in_w, 96)
            with pool.Fori(0, NQ) as q:
                inverse_deviation(q)
                nc.gpsimd.tensor_copy(ctx_hi[:], ctx_all[:, bass.ds(q * QK, QK)]).then_inc(s_ctxh, 1)
                wait_apart(pool, s_ctxh, q + 1)
                nc.gpsimd.tensor_tensor(ctx_lo[:], ctx_all[:, bass.ds(q * QK, QK)], ctx_hi[:].bitcast(F32),
                                        ALU.subtract).then_inc(s_ctx, 1)
            nc.gpsimd.tensor_tensor(xb[:], x_all, bo[:, None, :].to_broadcast([P, NB, D]), ALU.add).then_inc(s_pool, 1)
            pool.wait_ge(s_in_f, 80)
            nc.gpsimd.tensor_copy(w1_hi[:], w1s).then_inc(s_whi, 1)
            pool.wait_ge(s_in_w2, 16)
            nc.gpsimd.tensor_copy(w2_hi[:], w2s).then_inc(s_whi, 1)
            pool.wait_ge(s_whi, 2)
            nc.gpsimd.tensor_tensor(w1_lo[:], w1s, w1_hi[:].bitcast(F32), ALU.subtract).then_inc(s_fsplit, 1)
            nc.gpsimd.tensor_tensor(w2_lo[:], w2s, w2_hi[:].bitcast(F32), ALU.subtract).then_inc(s_fsplit, 1)
            with pool.Fori(0, NQ) as q:
                inverse_deviation(q + NQ)

            pool.wait_ge(s_cur3, NQ)
            pool.sem_inc(s_split, 2)
            pool.sem_inc(s_acc, 2)

            def spread(t, n):
                wait_apart(pool, s_row, 16 * (n + 1))
                nc.gpsimd.partition_broadcast(cw_all[:, t].rearrange("p e t -> p (e t)"), cw_row, P)\
                    .then_inc(s_cwb, 1)

            def accumulate(r, k):
                t, y = k // STEPS, 8 * r + k // FC
                pool.wait_ge(s_stt, 2 * y + 4)
                pool.wait_ge(s_acc, y + 2)
                nc.gpsimd.tensor_tensor(cur[:, t], cur[:, t], y_w[:, (k // FC) % 2], ALU.add).then_inc(s_acc, 1)

            def split(r, t):
                n = 2 * r + t
                wait_apart(pool, s_acc, 8 * r + 4 * t + 6)
                nc.gpsimd.tensor_copy(cur_hi[:, t], cur[:, t]).then_inc(s_chi, 1)
                pool.wait_ge(s_chi, n + 1)
                nc.gpsimd.tensor_tensor(cur_lo[:, t], cur[:, t], cur_hi[:, t].bitcast(F32), ALU.subtract)\
                    .then_inc(s_split, 1)

            def round_(r, last):
                for k in range(FC - 1, RS, FC):
                    if k == 15:
                        spread(1, 2 * r + 1)
                    if k == 31 and not last:
                        spread(0, 2 * r + 2)
                    accumulate(r, k)
                    if k % STEPS == STEPS - 1 and not last:
                        split(r, k // STEPS)

            spread(0, 0)
            with pool.Fori(0, R - 1) as r:
                round_(r, False)
            round_(R - 1, True)

        @block.scalar
        def _(act):
            with act.Fori(0, NQ) as q:
                act.wait_ge(s_xtp, q + 1)
                nc.scalar.activation(xt_hi, ps[:, 6], ACT.Copy).then_inc(s_xth, 1)
                act.wait_ge(s_qp, q + 1)
                nc.scalar.activation(q_full, ps[:, 7], ACT.Identity, bias=bqk[:, 0:1])
                nc.scalar.activation(q_hi[:, bass.ds(q * QUAD, QUAD)], ps[:, 7].rearrange("p (b s) -> p b s", s=S),
                                     ACT.Identity, bias=bqk[:, 0:1]).then_inc(s_qf, 1)
                act.wait_ge(s_kp, q + 1)
                nc.scalar.activation(k_full[:], ps[:, 4, 0:QK], ACT.Identity, bias=bqk[:, 1:2])
                nc.scalar.activation(k_hi[:, bass.ds(q * QUAD, QUAD), 0:KEYS],
                                     ps[:, 4, 0:QK].rearrange("p (b s) -> p b s", s=KEYS),
                                     ACT.Identity, bias=bqk[:, 1:2]).then_inc(s_kf, 1)

            def stack_q(b, slot):
                act.wait_ge(s_qsp, b + 1)
                nc.scalar.activation(q_stack[:, slot], ps[:, 6].rearrange("p (g s) -> p g s", s=S), ACT.Copy).then_inc(s_qs, 1)

            def exp(u, half):
                act.wait_ge(s_sub, u + 1)
                nc.scalar.activation(probs[:, half], probs[:, half], ACT.Exp, scale=SCALE).then_inc(s_exp, 1)

            def keep_probs_t(u, half):
                act.wait_ge(s_ptp, u + 1)
                nc.scalar.activation(probs_t[:, half], ps_pt, ACT.Copy).then_inc(s_pt, 1)

            def pair(p, last):
                for n in range(4):
                    u = 4 * p + n
                    if not (last and n == 3):
                        exp(u + 1, (n + 1) % 2)
                    keep_probs_t(u, n % 2)
                    if n % 2 == 0 and not (last and n == 2):
                        stack_q(2 * p + 1 + n // 2, (1 + n // 2) % 2)

            stack_q(0, 0)
            exp(0, 0)
            with act.Fori(0, NB // 2 - 1) as p:
                pair(p, False)
            pair(NB // 2 - 1, True)

            with act.Fori(0, NQ) as q:
                act.wait_ge(s_atp, q + 1)
                nc.scalar.activation(attn_t[:], ps[:, 6], ACT.Copy).then_inc(s_at, 1)
                act.wait_ge(s_ctp, q + 1)
                nc.scalar.activation(cur[:].rearrange("p t c -> p (t c)")[:, bass.ds(q * QT, QT)], ps[:, 5],
                                     ACT.Copy).then_inc(s_ct, 1)

            def hidden(m, c):
                act.wait_ge(s_w1, m + 1)
                if not (isinstance(m, int) and m < 2):
                    act.wait_ge(s_lo, m - 1)
                nc.scalar.activation(hid[:, c % 2], ps_h[:, c % 2], ACT.Gelu_apprx_tanh,
                                     bias=b1s[:, c:c + 1]).then_inc(s_gelu, 1)
                act.wait_ge(s_gelu, m + 1)
                nc.scalar.activation(hid_hi[:, c % RING], hid[:, c % 2], ACT.Copy).then_inc(s_hi, 1)

            def gate_tanh(n):
                act.wait_ge(s_arg, n + 1)
                nc.scalar.activation(tanh[:], arg[:], ACT.Tanh, scale=0.5).then_inc(s_tanh, 1)

            def round_(r, last):
                for k in range(RS):
                    if k == 11:
                        gate_tanh(2 * r + 1)
                    if k == 27 and not last:
                        gate_tanh(2 * r + 2)
                    if k + LAG < RS or not last:
                        hidden(RS * r + k + LAG, (k + LAG) % STEPS)

            gate_tanh(0)
            for m in range(LAG):
                hidden(m, m)
            with act.Fori(0, R - 1) as r:
                round_(r, False)
            round_(R - 1, True)

        @block.vector
        def _(dve):
            dve.wait_ge(s_in_w, 96)
            nc.vector.tensor_copy(wqkv_hi[:], wqkv[:]).then_inc(s_wsplit, 1)
            dve.wait_ge(s_wsplit, 1)
            nc.vector.tensor_tensor(wqkv_lo[:], wqkv[:], wqkv_hi[:].bitcast(F32), ALU.subtract).then_inc(s_wsplit, 1)

            def moments(n, src):
                for i in range(QUAD):
                    last = nc.vector.bn_stats(stats[:, i], src(i))
                last.then_inc(s_stats, 1)
                wait_apart(dve, s_stats, n + 1)
                for i in range(QUAD):
                    last = nc.vector.bn_aggr(mean_var[:, i], stats[:, i])
                last.then_inc(s_mv, 1)

            def normalise(n, src):
                dve.wait_ge(s_rstd, n + 1)
                for i in range(QUAD):
                    last = nc.vector.tensor_scalar(xn[:, i], src(i), mean_var[:, i, 0:1], rstd[:, i:i + 1],
                                                   ALU.subtract, ALU.mult)
                last.then_inc(s_xn, 1)

            dve.wait_ge(s_in_x, 16)
            dve.wait_ge(s_pool, 15)
            with dve.Fori(0, NQ) as q:
                def x_of(i):
                    return x_all[:, bass.ds(q * QUAD + i, 1)].rearrange("p b d -> p (b d)")
                moments(q, x_of)
                normalise(q, x_of)
                dve.wait_ge(s_xth, q + 1)
                nc.vector.tensor_tensor(xt_lo, ps[:, 6], xt_hi.bitcast(F32), ALU.subtract).then_inc(s_xtl, 1)
                dve.wait_ge(s_qf, q + 1)
                nc.vector.tensor_tensor(q_lo[:, bass.ds(q * QUAD, QUAD)], q_full.rearrange("p (b s) -> p b s", s=S),
                                        q_hi[:, bass.ds(q * QUAD, QUAD)].bitcast(F32), ALU.subtract).then_inc(s_ql, 1)
                dve.wait_ge(s_kf, q + 1)
                nc.vector.tensor_tensor(k_lo[:, bass.ds(q * QUAD, QUAD), 0:KEYS],
                                        k_full[:].rearrange("p (b s) -> p b s", s=KEYS),
                                        k_hi[:, bass.ds(q * QUAD, QUAD), 0:KEYS].bitcast(F32), ALU.subtract).then_inc(s_kl, 1)
                dve.wait_ge(s_vp, q + 1)
                for i in range(QUAD):
                    last = nc.vector.tensor_tensor(
                        v_one[:, bass.ds(q * QUAD + i, 1), :, 0:DH].rearrange("p b h d -> p (b h) d"),
                        ps[0:KEYS, 5, i * D:(i + 1) * D].rearrange("p (h d) -> p h d", d=DH),
                        bv[:].rearrange("p (h d) -> p h d", d=DH), ALU.add)
                last.then_inc(s_v, 1)

            def stack_k(b, slot):
                dve.wait_ge(s_ksp, b + 1)
                nc.vector.tensor_copy(k_stack[:, slot], ps_ks).then_inc(s_ks, 1)

            def softmax_shift(u, half):
                score = ps_score[:, 2 * half:2 * half + 2, 0:G * KPAD].rearrange("p j (g k) -> p j g k", k=KPAD)[:, :, :, 0:KEYS]
                dve.wait_ge(s_score, u + 1)
                nc.vector.tensor_reduce(top[:, half].rearrange("p (j g) -> p j g", g=G), score, AX_X, ALU.max).then_inc(s_top, 1)
                dve.wait_ge(s_top, u + 1)
                nc.vector.tensor_tensor(probs[:, half].rearrange("p (j g) k -> p j g k", g=G), score,
                                        top[:, half].rearrange("p (j g) -> p j g", g=G)[:, :, :, None].to_broadcast([P, 2, G, KEYS]),
                                        ALU.subtract).then_inc(s_sub, 1)

            def scale_values(b):
                dve.wait_ge(s_pv, 2 * b + 2)
                nc.vector.reciprocal(sum_inv[:], ps_o[:, :, DH]).then_inc(s_inv, 1)
                dve.wait_ge(s_inv, b + 1)
                at = attn[:, b] if isinstance(b, int) else attn[:, bass.ds(b, 1)].rearrange("p b d -> p (b d)")
                nc.vector.tensor_tensor(at.rearrange("p (h d) -> p h d", d=DH), ps_o[:, :, 0:DH],
                                        sum_inv[:, :, None].to_broadcast([P, H, DH]), ALU.mult).then_inc(s_attn, 1)

            def pair(p, first, last):
                for n in range(4):
                    softmax_shift(4 * p + n, n % 2)
                    if n % 2 == 0 and not (first and n == 0):
                        scale_values(2 * p - 1 + n // 2)
                    if n % 2 == 1 and not (last and n == 3):
                        stack_k(2 * p + 1 + n // 2, (1 + n // 2) % 2)

            stack_k(0, 0)
            pair(0, True, False)
            with dve.Fori(1, NB // 2 - 1) as p:
                pair(p, False, False)
            pair(NB // 2 - 1, False, True)
            scale_values(NB - 1)

            dve.wait_ge(s_pool, 16)
            with dve.Fori(0, NQ) as q:
                def x1_of(i):
                    return x1[:, bass.ds(q * QUAD + i, 1)].rearrange("p b d -> p (b d)")
                dve.wait_ge(s_op, q + 1)
                nc.vector.tensor_tensor(x1[:, bass.ds(q * QUAD, QUAD)], ps[:, 7].rearrange("p (b d) -> p b d", d=D),
                                        xb[:, bass.ds(q * QUAD, QUAD)], ALU.add).then_inc(s_x1, 1)
                wait_apart(dve, s_x1, q + 1)
                moments(NQ + q, x1_of)
                normalise(NQ + q, x1_of)
                dve.wait_ge(s_ct, q + 1)
                nc.vector.tensor_copy(cur_hi[:].rearrange("p t c -> p (t c)")[:, bass.ds(q * QT, QT)], ps[:, 5]).then_inc(s_chi3, 1)
                dve.wait_ge(s_chi3, q + 1)
                nc.vector.tensor_tensor(cur_lo[:].rearrange("p t c -> p (t c)")[:, bass.ds(q * QT, QT)], ps[:, 5],
                                        cur_hi[:].rearrange("p t c -> p (t c)")[:, bass.ds(q * QT, QT)].bitcast(F32),
                                        ALU.subtract).then_inc(s_cur3, 1)

            dve.sem_inc(s_stt, 2)

            GATE = 15

            def step(n, i, ins):
                ins.then_inc(s_gate, 1)
                dve.wait_ge(s_gate, GATE * n + i + 1)

            def gate_logits(n, r):
                dve.wait_ge(s_gl, n + 1)
                step(n, 0, nc.vector.tensor_tensor(
                    logit[:], ps[:, 6, 0:TG * E].rearrange("p (g e) -> p g e", e=E),
                    bgs[:, bass.ds(r * E, E)][:, None, :].to_broadcast([P, TG, E]), ALU.add))
                step(n, 1, nc.vector.tensor_tensor(hi2[:], logit[:, :, 0:2], logit[:, :, 2:4], ALU.max))
                step(n, 2, nc.vector.tensor_tensor(lo2[:], logit[:, :, 0:2], logit[:, :, 2:4], ALU.min))

            def gate_top2(n):
                step(n, 3, nc.vector.tensor_tensor(v12[:, 0], hi2[:, :, 0], hi2[:, :, 1], ALU.max))
                step(n, 4, nc.vector.tensor_tensor(v12[:, 1], hi2[:, :, 0], hi2[:, :, 1], ALU.min))
                step(n, 5, nc.vector.tensor_tensor(v12[:, 2], lo2[:, :, 0], lo2[:, :, 1], ALU.max))
                step(n, 6, nc.vector.tensor_tensor(v12[:, 3], v12[:, 1], v12[:, 2], ALU.max))

            def gate_args(n):
                step(n, 7, nc.vector.tensor_tensor(arg1[:], logit[:], v12[:, 0, :, None].to_broadcast([P, TG, E]), ALU.subtract))
                step(n, 8, nc.vector.tensor_tensor(arg[:], logit[:], v12[:, 3, :, None].to_broadcast([P, TG, E]), ALU.subtract))
                nc.vector.tensor_tensor(arg[:], arg[:], arg1[:], ALU.add).then_inc(s_arg, 1)

            def gate_beats(n):
                step(n, 9, nc.vector.tensor_tensor(
                    ge[:], logit[:, :, :, None].to_broadcast([P, TG, E, E]),
                    logit[:, :, None, :].to_broadcast([P, TG, E, E]), ALU.is_ge))
                step(n, 10, nc.vector.tensor_tensor(ge[:], ge[:], later[:], ALU.mult))
                step(n, 11, nc.vector.tensor_tensor(beat[:], ge[:], ge[:].rearrange("p g e j -> p g j e"), ALU.subtract))

            def gate_wins(n):
                step(n, 12, nc.vector.tensor_tensor(wins2[:], beat[:, :, :, 0:2], beat[:, :, :, 2:4], ALU.add))
                step(n, 13, nc.vector.tensor_tensor(wins[:], wins2[:, :, :, 0], wins2[:, :, :, 1], ALU.add))
                step(n, 14, nc.vector.tensor_tensor(wins[:], wins[:], wins_needed[:], ALU.is_ge))

            def gate_weights(n):
                dve.wait_ge(s_tanh, n + 1)
                nc.vector.tensor_scalar(tanh[:], tanh[:], 0.5, 0.5, ALU.mult, ALU.add).then_inc(s_tanh2, 1)
                dve.wait_ge(s_tanh2, n + 1)
                nc.vector.tensor_tensor(cw[:, 0:E * TG].rearrange("p (e g) -> p g e", e=E), tanh[:], wins[:],
                                        ALU.mult).then_inc(s_cw, 1)

            def gate_turned(n):
                dve.wait_ge(s_cwp, n + 1)
                nc.vector.tensor_copy(cw_t[:], ps[0:E * TG, 7, 0:P]).then_inc(s_cwt, 1)

            def hidden_low(m, c):
                dve.wait_ge(s_hi, m + 1)
                nc.vector.tensor_tensor(hid_lo[:, c % RING], hid[:, c % 2], hid_hi[:, c % RING].bitcast(F32),
                                        ALU.subtract).then_inc(s_lo, 1)

            def weigh(r, k):
                t, e, y = k // STEPS, k % STEPS // FC, 8 * r + k // FC
                dve.wait_ge(s_y, y + 1)
                dve.wait_ge(s_cwb, 2 * r + t + 1)
                dve.wait_ge(s_acc, y + 1)
                for h in range(2):
                    nc.vector.scalar_tensor_tensor(
                        y_w[:, (k // FC) % 2, h * HALF:(h + 1) * HALF], ps_y[:, h], b2s[:, e:e + 1],
                        cw_all[:, t, e, h * HALF:(h + 1) * HALF], ALU.add, ALU.mult).then_inc(s_stt, 1)

            def finish(n):
                dve.wait_ge(s_ftp, n + 1)
                nc.vector.tensor_tensor(xb[:, 4 * n:4 * n + 4], ps[:, 6 + n % 2].rearrange("p (b d) -> p b d", d=D),
                                        x1[:, 4 * n:4 * n + 4], ALU.add).then_inc(s_fin, 1)

            def round_(r, last):
                for k in range(RS):
                    for t, n, rn, k0 in ((1, 2 * r + 1, r, 0), (0, 2 * r + 2, r + 1, STEPS)):
                        if k0 and last:
                            continue
                        if k == k0 + 7:
                            gate_logits(n, rn)
                        if k == k0 + 8:
                            gate_top2(n)
                        if k == k0 + 9:
                            gate_args(n)
                        if k == k0 + 10:
                            gate_beats(n)
                        if k == k0 + 11:
                            gate_wins(n)
                        if k == k0 + 12:
                            gate_weights(n)
                        if k == k0 + 13:
                            gate_turned(n)
                    if k % FC == FC - 1:
                        weigh(r, k)
                    if last and k == STEPS + 4:
                        finish(0)
                        finish(1)
                    if k + LAG - 1 < RS or not last:
                        hidden_low(RS * r + k + LAG - 1, (k + LAG - 1) % STEPS)

            gate_logits(0, 0)
            gate_top2(0)
            gate_args(0)
            gate_beats(0)
            gate_wins(0)
            gate_weights(0)
            gate_turned(0)
            for m in range(LAG - 1):
                hidden_low(m, m)
            with dve.Fori(0, R - 1) as r:
                round_(r, False)
            round_(R - 1, True)
            finish(2)
            finish(3)

        @block.tensor
        def _(pe):
            def product(dst, w_hi, w_lo, a_hi, a_lo, start=True, stop=True):
                nc.tensor.matmul(dst, w_hi, a_lo, start=start, stop=False)
                nc.tensor.matmul(dst, w_lo, a_hi, start=False, stop=False)
                return nc.tensor.matmul(dst, w_hi, a_hi, start=False, stop=stop)

            pe.wait_ge(s_ident, 1)
            pe.wait_ge(s_wsplit, 2)
            with pe.Fori(0, NQ) as q:
                pe.wait_ge(s_xn, q + 1)
                for i in range(QUAD):
                    last = nc.tensor.transpose(ps[:, 6, i * S:(i + 1) * S], xn[:, i], ident[:])
                last.then_inc(s_xtp, 1)
                pe.wait_ge(s_ctx, q + 1)
                product(ps[:, 4, 0:QK], wqkv_hi[:, 1], wqkv_lo[:, 1], ctx_hi[:], ctx_lo[:]).then_inc(s_kp, 1)
                for i in range(QUAD):
                    keys = slice(i * KEYS, (i + 1) * KEYS)
                    last = product(ps[0:KEYS, 5, i * D:(i + 1) * D], ctx_hi[:, keys], ctx_lo[:, keys],
                                   wqkv_hi[:, 2], wqkv_lo[:, 2])
                last.then_inc(s_vp, 1)
                pe.wait_ge(s_xtl, q + 1)
                product(ps[:, 7], wqkv_hi[:, 0], wqkv_lo[:, 0], xt_hi, xt_lo).then_inc(s_qp, 1)

            def stack_heads(b, parts, kind, dst, done):
                for g in range(G):
                    for part in range(2):
                        last = nc.tensor.matmul(dst[:, g], sel[:, kind + part, g],
                                                parts[part][:, bass.ds(b, 1)].rearrange("p b s -> p (b s)"),
                                                start=(part == 0), stop=(part == 1))
                last.then_inc(done, 1)

            def stack_q(b):
                stack_heads(b, (q_hi, q_lo), 0, ps[:, 6].rearrange("p (g s) -> p g s", s=S), s_qsp)

            def stack_k(b):
                stack_heads(b, (k_hi, k_lo), 2, ps_ks, s_ksp)

            def scores(u, b, half, slot):
                if half == 0:
                    pe.wait_ge(s_qs, b + 1)
                    pe.wait_ge(s_ks, b + 1)
                if not (isinstance(u, int) and u < 2):
                    pe.wait_ge(s_sub, u - 1)
                for g in range(G):
                    for j in (2 * half, 2 * half + 1):
                        last = nc.tensor.matmul(ps_score[:, j, g * KPAD:(g + 1) * KPAD],
                                                q_stack[32 * j:32 * j + 32, slot, g], k_stack[32 * j:32 * j + 32, slot, g],
                                                start=True, stop=True)
                last.then_inc(s_score, 1)

            def turn_probs(u, half):
                pe.wait_ge(s_exp, u + 1)
                if not (isinstance(u, int) and u < 1):
                    pe.wait_ge(s_pt, u)
                for i in range(HH):
                    last = nc.tensor.transpose(ps_pt[:, i], probs[:, half, i], ident[:])
                last.then_inc(s_ptp, 1)

            def values(u, b, half):
                pe.wait_ge(s_pt, u + 1)
                if half == 0 and not (isinstance(b, int) and b < 1):
                    pe.wait_ge(s_attn, b)
                for i in range(HH):
                    h = half * HH + i
                    last = nc.tensor.matmul(ps_o[:, h], probs_t[:, half, i],
                                            v_one[:, bass.ds(b, 1), h].rearrange("p b d -> p (b d)"), start=True, stop=True)
                last.then_inc(s_pv, 1)

            def pair(p, last):
                for n in range(4):
                    u = 4 * p + n
                    if not (last and n == 3):
                        turn_probs(u + 1, (n + 1) % 2)
                    if n % 2 == 0 and not (last and n == 2):
                        stack_q(2 * p + 1 + n // 2)
                    values(u, 2 * p + n // 2, n % 2)
                    if n % 2 == 0 and not (last and n == 2):
                        stack_k(2 * p + 1 + n // 2)
                    if not (last and n >= 2):
                        scores(u + 2, 2 * p + n // 2 + 1, n % 2, (n // 2 + 1) % 2)

            pe.wait_ge(s_sel, 1)
            pe.wait_ge(s_ql, NQ)
            pe.wait_ge(s_kl, NQ)
            pe.wait_ge(s_v, NQ)
            stack_q(0)
            stack_k(0)
            scores(0, 0, 0, 0)
            scores(1, 0, 1, 0)
            turn_probs(0, 0)
            pair(0, False)
            with pe.Fori(1, NB // 2 - 1) as p:
                pair(p, False)
            pair(NB // 2 - 1, True)

            pe.wait_ge(s_attn, NB)
            for q in range(NQ):
                for i in range(QUAD):
                    last = nc.tensor.transpose(ps[:, 6, i * S:(i + 1) * S],
                                               attn[:, q * QUAD + i], ident[:])
                last.then_inc(s_atp, 1)
                pe.wait_ge(s_at, q + 1)
                for i in range(QUAD):
                    last = nc.tensor.matmul(ps[:, 7, i * D:(i + 1) * D], attn_t[:, i * S:(i + 1) * S], wo[:],
                                            start=True, stop=True)
                last.then_inc(s_op, 1)
                pe.wait_ge(s_xn, NQ + q + 1)
                for i in range(QUAD):
                    last = nc.tensor.transpose(ps[:, 5, i * S:(i + 1) * S], xn[:, i], ident[:])
                last.then_inc(s_ctp, 1)

            def gate(t, n, r):
                pe.wait_ge(s_split, n + 1)
                for i in range(TG):
                    last = nc.tensor.matmul(ps[:, 6, i * E:(i + 1) * E], cur[:, t, i * P:(i + 1) * P],
                                            wgs[:, bass.ds(r * E, E)], start=True, stop=True)
                last.then_inc(s_gl, 1)

            def turn_gate(n):
                pe.wait_ge(s_cw, n + 1)
                nc.tensor.transpose(ps[:, 7, 0:P], cw[:], ident[:]).then_inc(s_cwp, 1)

            def first(m, c, t, n, wait_slot=True):
                if c == 0:
                    pe.wait_ge(s_split, n + 1)
                if wait_slot:
                    pe.wait_ge(s_gelu, m - 1)
                w = slice(c * P, (c + 1) * P)
                for h in range(2):
                    cols = slice(h * HALF, (h + 1) * HALF)
                    last = product(ps_h[:, c % 2, cols], w1_hi[:, w], w1_lo[:, w], cur_hi[:, t, cols], cur_lo[:, t, cols])
                last.then_inc(s_w1, 1)

            def second(r, k):
                c, y = k % STEPS, 8 * r + k // FC
                pe.wait_ge(s_lo, RS * r + k + 1)
                w = slice(c * P, (c + 1) * P)
                for h in range(2):
                    if c % FC == 0:
                        pe.wait_ge(s_stt, 2 * y + h + 1)
                    cols = slice(h * HALF, (h + 1) * HALF)
                    last = product(ps_y[:, h], w2_hi[:, w], w2_lo[:, w], hid_hi[:, c % RING, cols],
                                   hid_lo[:, c % RING, cols], c % FC == 0, c % FC == FC - 1)
                if c % FC == FC - 1:
                    last.then_inc(s_y, 1)

            def turn_back(n):
                t = n // 2
                pe.wait_ge(s_acc, 8 * (R - 1) + 4 * t + 6)
                for i in range(4):
                    c = (n % 2) * 4 + i
                    last = nc.tensor.transpose(ps[:, 6 + n % 2, i * P:(i + 1) * P], cur[:, t, c * P:(c + 1) * P], ident[:])
                last.then_inc(s_ftp, 1)

            def round_(r, last):
                for k in range(RS):
                    if k == 6:
                        gate(1, 2 * r + 1, r)
                    if k == 22 and not last:
                        gate(0, 2 * r + 2, r + 1)
                    if k == 13:
                        turn_gate(2 * r + 1)
                    if k == 29 and not last:
                        turn_gate(2 * r + 2)
                    if last and k == STEPS + 3:
                        turn_back(0)
                        turn_back(1)
                    second(r, k)
                    a = k + LAG
                    if a < RS:
                        first(RS * r + a, a % STEPS, a // STEPS, 2 * r + a // STEPS)
                    elif not last:
                        first(RS * r + a, a % STEPS, 0, 2 * r + 2)

            pe.wait_ge(s_fsplit, 2)
            gate(0, 0, 0)
            for m in range(LAG):
                first(m, m, 0, 0, wait_slot=(m >= 2))
            turn_gate(0)
            with pe.Fori(0, R - 1) as r:
                round_(r, False)
            round_(R - 1, True)
            turn_back(2)
            turn_back(3)


def kernel(x, ctx_1024, L0_xattn_wq, L0_xattn_bq, L0_xattn_wk, L0_xattn_bk, L0_xattn_wv, L0_xattn_bv, L0_xattn_wo,
           L0_xattn_bo, L0_ffn_Wg, L0_ffn_bg, L0_ffn_W1, L0_ffn_b1, L0_ffn_W2, L0_ffn_b2):
    import numpy as np
    import concourse.bacc as bacc
    from concourse.bass_utils import run_bass_kernel_spmd

    def laid(a):
        return np.ascontiguousarray(a)

    D = x.shape[-1]
    ctx = np.asarray(ctx_1024)
    arrays = {
        "x": laid(x),
        "ctx_t": laid(ctx.reshape(-1, D).T),
        "w_qkv": laid(np.stack([np.asarray(w).T for w in (L0_xattn_wq, L0_xattn_wk, L0_xattn_wv)], axis=1)),
        "w_o": laid(np.asarray(L0_xattn_wo).T),
        "b_qk": laid(np.stack([np.asarray(L0_xattn_bq), np.asarray(L0_xattn_bk)], axis=1)),
        "b_v": laid(L0_xattn_bv),
        "b_o": laid(L0_xattn_bo),
        "wg": laid(np.asarray(L0_ffn_Wg).transpose(1, 0, 2).reshape(D, -1)),
        "bg": laid(np.asarray(L0_ffn_bg).reshape(-1)),
        "w1": laid(L0_ffn_W1),
        "b1": laid(np.asarray(L0_ffn_b1).reshape(-1, 128).T),
        "w2": laid(np.asarray(L0_ffn_W2).reshape(-1, D)),
        "b2": laid(np.asarray(L0_ffn_b2).T),
    }
    nc = bacc.Bacc("TRN2", target_bir_lowering=False, num_devices=1)
    args = [nc.dram_tensor(f"in_{name}", a.shape, mybir.dt.from_np(a.dtype), kind="ExternalInput").ap()
            for name, a in arrays.items()]
    out = nc.dram_tensor("out_0", arrays["x"].shape, F32, kind="ExternalOutput").ap()
    xattn_moe(nc, *args, out)
    r = run_bass_kernel_spmd(nc, [{f"in_{name}": a for name, a in arrays.items()}], core_ids=[0])
    return r.results[0]["out_0"]
```

```python
from contextlib import ExitStack

import concourse.bass as bass
from concourse import mybir

F32 = mybir.dt.float32
F32R = mybir.dt.float32r
BF16 = mybir.dt.bfloat16
F16 = mybir.dt.float16
ALU = mybir.AluOpType
ACT = mybir.ActivationFunctionType
AX_X = mybir.AxisListType.X

P = 128
EPS = 1e-5


def xattn_moe(nc, x, ctx_t, w_qkv, w_o, b_qk, b_v, b_o, wg, bg, w1, b1, w2, b2, out):
    NB, S, D = x.shape
    KEYS = ctx_t.shape[1] // NB
    KPAD = KEYS + KEYS % 2
    H, DH = 16, 8
    G, J = 4, 4
    QUAD = 4
    QT, QK = QUAD * S, QUAD * KEYS
    NQ = NB // QUAD
    HH = H // 2
    E, R = b2.shape[1], wg.shape[1] // b2.shape[1]
    FC = b1.shape[1] // E
    T = NB * S // 2
    TG = T // P
    STEPS = E * FC
    RS = 2 * STEPS
    HALF = 512
    LAG = 3
    RING = 4
    SCALE = float(DH) ** -0.5
    PSCALE = 2.0 ** 14
    POOL_CONSTANTS = 15

    with ExitStack() as stack:
        def sb(name, shape, dt=F32):
            return stack.enter_context(nc.sbuf_tensor(name, shape, dt))

        def sem(name):
            return stack.enter_context(nc.semaphore(name))

        ident = sb("ident", [P, P])
        wqkv = sb("wqkv", [P, 3, D])
        wqkv_hi = sb("wqkv_hi", [P, 3, D], F32R)
        wqkv_lo = sb("wqkv_lo", [P, 3, D], F32R)
        wo = sb("wo", [P, D])
        bqk = sb("bqk", [P, 2])
        bv = sb("bv", [KEYS, D])
        bo = sb("bo", [P, D])
        head_mask = sb("head_mask", [P, J])
        wgs = sb("wgs", [P, R * E])
        bgs = sb("bgs", [P, R * E])
        w1_hi = sb("w1_hi", [P, STEPS * P], F32R)
        w1_lo = sb("w1_lo", [P, STEPS * P], F32R)
        w2_hi = sb("w2_hi", [P, STEPS * P], F32R)
        w2_lo = sb("w2_lo", [P, STEPS * P], F32R)
        b1s = sb("b1s", [P, STEPS])
        b2s = sb("b2s", [P, E])
        minus_half = sb("minus_half", [P, NB])
        later = sb("later", [P, TG, E, E])
        wins_needed = sb("wins_needed", [P, TG, E])
        xb = sb("xb", [P, NB, D])
        ctx_all = sb("ctx_all", [P, NB * KEYS])
        stats = sb("stats", [P, NB, 6])
        mean_var = sb("mean_var", [P, NB, 2])
        var_eps = sb("var_eps", [P, NB])
        rstd = sb("rstd", [P, NB])
        xn = sb("xn", [P, 2, QUAD, D])
        attn_t = ctx_all[:, 0:2 * QT].rearrange("p (s c) -> p s c", s=2)
        q_slot = sb("q_slot", [P, 2, 2, S], F32R)
        k_slot = sb("k_slot", [P, 2, 2, J, KPAD], F32R)
        v_slot = sb("v_slot", [KEYS, 2, H * 3 * (DH + 1)], BF16)
        top = sb("top", [P, 2, HH])
        summed = sb("summed", [P, H, DH + 1])
        sum_inv = sb("sum_inv", [P, H])
        x1 = sb("x1", [P, NB, D])
        cur = sb("cur", [P, 2, T])

        def parts_of(whole, *sizes):
            at = [sum(sizes[:i]) for i in range(len(sizes) + 1)]
            assert at[-1] <= whole.shape[1]
            return [whole[:, a:b] for a, b in zip(at, at[1:])]

        shared_r = sb("shared_r", [P, 2 * RING * T], F32R)
        q_hi, q_lo, k_hi, k_lo = parts_of(shared_r, NB * S, NB * S, NB * KPAD, NB * KPAD)
        q_hi, q_lo, k_hi, k_lo = (a.rearrange("p (b s) -> p b s", b=NB) for a in (q_hi, q_lo, k_hi, k_lo))
        hid_hi, hid_lo = (a.rearrange("p (s t) -> p s t", s=RING) for a in parts_of(shared_r, RING * T, RING * T))
        shared = sb("shared", [P, 2 * E * T])
        v_parts, probs, probs_t, v_full = parts_of(shared, NB * H * 3 * (DH + 1) // 2, H * KEYS, 2 * HH * S, 2 * QT)
        v_parts = v_parts[0:KEYS].bitcast(BF16).rearrange("p (b h c d) -> p b h c d", b=NB, h=H, c=3)
        probs = probs.rearrange("p (s h k) -> p s h k", s=2, h=HH)
        probs_t = probs_t[0:KEYS].bitcast(F16).rearrange("p (s c h t) -> p s c h t", s=2, c=2, h=HH)
        v_full = v_full[0:KEYS].rearrange("p (s c) -> p s c", s=2)
        attn = cur[:].rearrange("p t (b d) -> p (t b) d", d=D)
        cw_all = shared[:].rearrange("p (t e c) -> p t e c", t=2, e=E)
        w12s = sb("w12s", [P, 2 * STEPS * P])
        w1s, w2s = parts_of(w12s, STEPS * P, STEPS * P)
        cw_row = w12s[0:1, 0:E * T]
        hid_or = sb("hid_or", [P, 2 * T])
        hid = hid_or[:].rearrange("p (s t) -> p s t", s=2)
        q_full, k_full = parts_of(hid_or, 2 * QT, 2 * QK)
        q_full, k_full = q_full.rearrange("p (s c) -> p s c", s=2), k_full.rearrange("p (s c) -> p s c", s=2)
        curs_r = sb("curs_r", [P, 4 * T], F32R)
        cur_hi, cur_lo = (a.rearrange("p (t c) -> p t c", t=2) for a in parts_of(curs_r, 2 * T, 2 * T))
        xt_hi, xt_lo = (a.rearrange("p (s c) -> p s c", s=2) for a in parts_of(curs_r, 2 * QT, 2 * QT))
        ctx_r = sb("ctx_r", [P, 2 * NB * KEYS], F32R)
        ctx_hi, ctx_lo = parts_of(ctx_r, NB * KEYS, NB * KEYS)
        x_or_y = sb("x_or_y", [P, NB * D])
        x_all = x_or_y[:].rearrange("p (b d) -> p b d", b=NB)
        y_w = x_or_y[:].rearrange("p (s t) -> p s t", s=2)

        ps = stack.enter_context(nc.psum_tensor("ps", [P, 8, 512], F32))
        ps_score = ps[:, 0:4]
        ps_pt = ps[0:KEYS, 4:6].rearrange("p b (h s) -> p (b h) s", s=S)
        ps_o = ps[:, 6:8, 0:H * 3 * (DH + 1)].rearrange("p b (h c d) -> p b h c d", c=3, d=DH + 1)

        s_in_x = [sem(f"s_in_x{q}") for q in range(NQ)]
        s_in_w, s_in_f, s_in_w2 = sem("s_in_w"), sem("s_in_f"), sem("s_in_w2")
        s_ident, s_pool, s_mask, s_wsplit, s_fsplit = sem("s_ident"), sem("s_pool"), sem("s_mask"), sem("s_wsplit"), sem("s_fsplit")
        s_whi, s_unread, s_xb = sem("s_whi"), sem("s_unread"), sem("s_xb")
        s_stats, s_mv, s_ve, s_rstd, s_xn = sem("s_stats"), sem("s_mv"), sem("s_ve"), sem("s_rstd"), sem("s_xn")
        s_xtp, s_xth, s_xtl = sem("s_xtp"), sem("s_xth"), sem("s_xtl")
        s_qp, s_qf, s_ql = sem("s_qp"), sem("s_qf"), sem("s_ql")
        s_ctxh, s_ctx, s_kp, s_kf, s_kl = sem("s_ctxh"), sem("s_ctx"), sem("s_kp"), sem("s_kf"), sem("s_kl")
        s_vp, s_vf, s_vsplit, s_v = sem("s_vp"), sem("s_vf"), sem("s_vsplit"), sem("s_v")
        s_qk_slot, s_v_slot = sem("s_qk_slot"), sem("s_v_slot")
        s_score, s_top, s_sub, s_exp = sem("s_score"), sem("s_top"), sem("s_sub"), sem("s_exp")
        s_ptp, s_pth, s_pt, s_osum = sem("s_ptp"), sem("s_pth"), sem("s_pt"), sem("s_osum")
        s_pv, s_inv, s_attn = sem("s_pv"), sem("s_inv"), sem("s_attn")
        s_atp, s_at, s_op, s_x1 = sem("s_atp"), sem("s_at"), sem("s_op"), sem("s_x1")
        s_ctp, s_ct, s_chi3, s_cur3 = sem("s_ctp"), sem("s_ct"), sem("s_chi3"), sem("s_cur3")
        s_w1, s_gelu, s_hi, s_lo = sem("s_w1"), sem("s_gelu"), sem("s_hi"), sem("s_lo")
        s_y, s_stt, s_acc, s_chi, s_split = sem("s_y"), sem("s_stt"), sem("s_acc"), sem("s_chi"), sem("s_split")
        s_tanh2 = sem("s_tanh2")
        s_gl, s_gate, s_arg, s_tanh, s_cw = sem("s_gl"), sem("s_gate"), sem("s_arg"), sem("s_tanh"), sem("s_cw")
        s_cwp, s_cwt, s_row, s_cwb = sem("s_cwp"), sem("s_cwt"), sem("s_row"), sem("s_cwb")
        s_ftp, s_fin, s_out = sem("s_ftp"), sem("s_fin"), sem("s_out")

        logit = sb("logit", [P, TG, E])
        hi2 = sb("hi2", [P, TG, 2])
        lo2 = sb("lo2", [P, TG, 2])
        v12 = sb("v12", [P, 4, TG])
        ge = sb("ge", [P, TG, E, E])
        beat = sb("beat", [P, TG, E, E])
        wins2 = sb("wins2", [P, TG, E, 2])
        wins = sb("wins", [P, TG, E])
        arg1 = sb("arg1", [P, TG, E])
        arg = sb("arg", [P, TG, E])
        tanh = sb("tanh", [P, TG, E])
        cw = sb("cw", [P, P])
        cw_t = sb("cw_t", [E * TG, P])
        ps_h = ps[:, 0:4].rearrange("p (s b) c -> p s (b c)", s=2)
        ps_y = ps[:, 4:6]

        block = stack.enter_context(nc.Block())

        def wait_apart(eng, semaphore, value):
            eng.wait_ge(semaphore, value)
            eng.sem_inc(s_unread, 1)

        @block.sync
        def _(sp):
            for q in range(NQ):
                quad = slice(q * QUAD, (q + 1) * QUAD)
                sp.dma_start(x_all[:, quad], x.rearrange("b s d -> s b d")[:, quad]).then_inc(s_in_x[q], 16)
            for dst, src in ((wqkv[:], w_qkv), (ctx_all[:], ctx_t), (wo[:], w_o), (bqk[:], b_qk),
                             (bv[:], b_v[None, :].to_broadcast([KEYS, D])), (bo[:], b_o[None, :].to_broadcast([P, D]))):
                sp.dma_start(dst, src).then_inc(s_in_w, 16)
            sp.dma_start(w1s.rearrange("p (e f) -> p e f", e=E), w1.rearrange("e h f -> h e f")).then_inc(s_in_f, 16)
            for dst, src in ((wgs[:], wg), (bgs[:], bg[None, :].to_broadcast([P, R * E])), (b1s[:], b1), (b2s[:], b2)):
                sp.dma_start(dst, src).then_inc(s_in_f, 16)
            sp.dma_start(w2s.rearrange("p (c h) -> p c h", h=D), w2.rearrange("(c p) h -> p c h", p=P)).then_inc(s_in_w2, 16)

            def row(n):
                sp.wait_ge(s_cwt, n + 1)
                sp.dma_start(cw_row, cw_t[:]).then_inc(s_row, 16)

            row(0)
            with sp.Fori(0, R - 1) as r:
                row(2 * r + 1)
                row(2 * r + 2)
            row(2 * R - 1)
            for t in range(2):
                for i in range(2):
                    n = 2 * t + i
                    sp.wait_ge(s_fin, n + 1)
                    sp.dma_start(out.rearrange("b s d -> s b d")[:, 4 * n:4 * n + 4],
                                 xb[:, 4 * n:4 * n + 4]).then_inc(s_out, 16)
            sp.wait_ge(s_out, 64)

        @block.gpsimd
        def _(pool):
            nc.gpsimd.memset(ident[:], 0.0).then_inc(s_pool, 1)
            nc.gpsimd.memset(later[:], 0.0).then_inc(s_pool, 1)
            pool.wait_ge(s_pool, 2)
            nc.gpsimd.affine_select(out=ident[:], in_=ident[:], compare_op=ALU.not_equal, fill=1.0, base=0,
                                    pattern=[[-1, P]], channel_multiplier=1).then_inc(s_ident, 1)
            nc.gpsimd.memset(v_parts[:, :, :, 0, DH], 1.0).then_inc(s_pool, 1)
            nc.gpsimd.memset(v_parts[:, :, :, 1:3, DH], 0.0).then_inc(s_pool, 1)
            nc.gpsimd.memset(k_hi.bitcast(F32), 0.0).then_inc(s_pool, 1)
            nc.gpsimd.memset(k_lo.bitcast(F32), 0.0).then_inc(s_pool, 1)
            nc.gpsimd.memset(minus_half[:], -0.5).then_inc(s_pool, 1)
            nc.gpsimd.memset(cw[:], 0.0).then_inc(s_pool, 1)
            for e in range(E):
                nc.gpsimd.memset(wins_needed[:, :, e], 2.0 - e).then_inc(s_pool, 1)
                if e < E - 1:
                    nc.gpsimd.memset(later[:, :, e, e + 1:E], 1.0).then_inc(s_pool, 1)

            def inverse_deviation(n, q):
                quad = slice(q * QUAD, (q + 1) * QUAD)
                pool.wait_ge(s_mv, n + 1)
                nc.gpsimd.tensor_scalar(var_eps[:, quad], mean_var[:, quad, 1], EPS, 1.0, ALU.add, ALU.mult).then_inc(s_ve, 1)
                pool.wait_ge(s_ve, n + 1)
                nc.gpsimd.tensor_tensor(rstd[:, quad], var_eps[:, quad], minus_half[:, quad], ALU.pow).then_inc(s_rstd, 1)

            pool.wait_ge(s_in_w, 96)
            nc.gpsimd.tensor_copy(ctx_hi, ctx_all[:]).then_inc(s_ctxh, 1)
            inverse_deviation(0, 0)
            pool.wait_ge(s_ctxh, 1)
            nc.gpsimd.tensor_tensor(ctx_lo, ctx_all[:], ctx_hi.bitcast(F32), ALU.subtract).then_inc(s_ctx, 1)
            for q in range(1, NQ):
                inverse_deviation(q, q)
            for q in range(NQ):
                pool.wait_ge(s_vf, q + 1)
                full = v_full[:, q % 2].rearrange("p (b h d) -> p b h d", b=QUAD, h=H)
                parts = [v_parts[:, q * QUAD:(q + 1) * QUAD, :, c, 0:DH] for c in range(3)]
                for c in range(2):
                    nc.gpsimd.tensor_copy(parts[c], full).then_inc(s_vsplit, 1)
                    pool.wait_ge(s_vsplit, 4 * q + 2 * c + 1)
                    nc.gpsimd.tensor_tensor(full, full, parts[c], ALU.subtract).then_inc(s_vsplit, 1)
                    pool.wait_ge(s_vsplit, 4 * q + 2 * c + 2)
                nc.gpsimd.tensor_copy(parts[2], full).then_inc(s_v, 1)

            def slots(b, slot):
                one = bass.ds(b, 1)
                for part, k in ((0, k_hi), (1, k_lo)):
                    nc.gpsimd.tensor_tensor(k_slot[:, slot, part], k[:, one].bitcast(F32).to_broadcast([P, J, KPAD]),
                                            head_mask[:, :, None].to_broadcast([P, J, KPAD]), ALU.mult).then_inc(s_qk_slot, 1)
                for part, q in ((0, q_hi), (1, q_lo)):
                    nc.gpsimd.tensor_copy(q_slot[:, slot, part], q[:, one].bitcast(F32).rearrange("p b s -> p (b s)"))\
                        .then_inc(s_qk_slot, 1)
                nc.gpsimd.tensor_copy(v_slot[:, slot], v_parts[:, one].rearrange("p b h c d -> p (b h c d)")).then_inc(s_v_slot, 1)

            pool.wait_ge(s_mask, 1)
            pool.wait_ge(s_ql, NQ)
            pool.wait_ge(s_kl, NQ)
            slots(0, 0)
            slots(1, 1)
            nc.gpsimd.tensor_tensor(xb[:], x_all, bo[:, None, :].to_broadcast([P, NB, D]), ALU.add).then_inc(s_xb, 1)
            pool.wait_ge(s_whi, 2)
            nc.gpsimd.tensor_tensor(w1_lo[:], w1s, w1_hi[:].bitcast(F32), ALU.subtract).then_inc(s_fsplit, 1)
            nc.gpsimd.tensor_tensor(w2_lo[:], w2s, w2_hi[:].bitcast(F32), ALU.subtract).then_inc(s_fsplit, 1)
            with pool.Fori(1, NB // 2) as p:
                for i in range(2):
                    wait_apart(pool, s_pv, 4 * p + 2 * i - 2)
                    slots(2 * p + i, i)
            for q in range(NQ):
                inverse_deviation(NQ + q, q)

            pool.wait_ge(s_cur3, NQ)
            pool.sem_inc(s_split, 2)
            pool.sem_inc(s_acc, 2)

            def spread(t, n):
                wait_apart(pool, s_row, 16 * (n + 1))
                nc.gpsimd.partition_broadcast(cw_all[:, t].rearrange("p e t -> p (e t)"), cw_row, P)\
                    .then_inc(s_cwb, 1)

            def accumulate(r, k):
                t, y = k // STEPS, 8 * r + k // FC
                pool.wait_ge(s_stt, 2 * y + 4)
                pool.wait_ge(s_acc, y + 2)
                nc.gpsimd.tensor_tensor(cur[:, t], cur[:, t], y_w[:, (k // FC) % 2], ALU.add).then_inc(s_acc, 1)

            def split(r, t):
                n = 2 * r + t
                wait_apart(pool, s_acc, 8 * r + 4 * t + 6)
                nc.gpsimd.tensor_copy(cur_hi[:, t], cur[:, t]).then_inc(s_chi, 1)
                pool.wait_ge(s_chi, n + 1)
                nc.gpsimd.tensor_tensor(cur_lo[:, t], cur[:, t], cur_hi[:, t].bitcast(F32), ALU.subtract)\
                    .then_inc(s_split, 1)

            def round_(r, last):
                for k in range(FC - 1, RS, FC):
                    if k == 15:
                        spread(1, 2 * r + 1)
                    if k == 31 and not last:
                        spread(0, 2 * r + 2)
                    accumulate(r, k)
                    if k % STEPS == STEPS - 1 and not last:
                        split(r, k // STEPS)

            spread(0, 0)
            with pool.Fori(0, R - 1) as r:
                round_(r, False)
            round_(R - 1, True)

        @block.scalar
        def _(act):
            act.wait_ge(s_pool, POOL_CONSTANTS)
            for i in range(NQ + 1):
                if i < NQ:
                    quad = slice(i * QUAD, (i + 1) * QUAD)
                    act.wait_ge(s_kp, i + 1)
                    if i >= 2:
                        act.wait_ge(s_kl, i - 1)
                    nc.scalar.activation(k_full[:, i % 2], ps[:, 2 + i % 2, 0:QK], ACT.Identity, bias=bqk[:, 1:2])
                    nc.scalar.activation(k_hi[:, quad, 0:KEYS], ps[:, 2 + i % 2, 0:QK].rearrange("p (b s) -> p b s", s=KEYS),
                                         ACT.Identity, bias=bqk[:, 1:2]).then_inc(s_kf, 1)
                    act.wait_ge(s_xtp, i + 1)
                    if i >= 2:
                        act.wait_ge(s_qp, i - 1)
                    nc.scalar.activation(xt_hi[:, i % 2], ps[:, i % 2], ACT.Copy).then_inc(s_xth, 1)
                if i >= 1:
                    q = i - 1
                    act.wait_ge(s_qp, q + 1)
                    if q >= 2:
                        act.wait_ge(s_ql, q - 1)
                    nc.scalar.activation(q_full[:, q % 2], ps[:, 6 + q % 2], ACT.Identity, bias=bqk[:, 0:1])
                    nc.scalar.activation(q_hi[:, q * QUAD:i * QUAD], ps[:, 6 + q % 2].rearrange("p (b s) -> p b s", s=S),
                                         ACT.Identity, bias=bqk[:, 0:1]).then_inc(s_qf, 1)

            def exp(u, half):
                act.wait_ge(s_sub, u + 1)
                nc.scalar.activation(probs[:, half], probs[:, half], ACT.Exp, scale=SCALE).then_inc(s_exp, 1)

            def keep_probs_t(u, half):
                act.wait_ge(s_ptp, u + 1)
                if not (isinstance(u, int) and u < 2):
                    act.wait_ge(s_pv, u - 1)
                nc.scalar.activation(probs_t[:, half, 0], ps_pt, ACT.Copy, scale=PSCALE).then_inc(s_pth, 1)

            def pair(p, last):
                for n in range(4):
                    u = 4 * p + n
                    if not (last and n == 3):
                        exp(u + 1, (n + 1) % 2)
                    keep_probs_t(u, n % 2)

            exp(0, 0)
            act.wait_ge(s_in_f, 80)
            nc.scalar.activation(w1_hi[:], w1s, ACT.Copy).then_inc(s_whi, 1)
            act.wait_ge(s_in_w2, 16)
            nc.scalar.activation(w2_hi[:], w2s, ACT.Copy).then_inc(s_whi, 1)
            pair(0, False)
            with act.Fori(1, NB // 2 - 1) as p:
                pair(p, False)
            pair(NB // 2 - 1, True)

            for i in range(NQ + 2):
                if i < NQ:
                    act.wait_ge(s_atp, i + 1)
                    if i >= 2:
                        act.wait_ge(s_op, i - 1)
                    nc.scalar.activation(attn_t[:, i % 2], ps[:, i % 2], ACT.Copy).then_inc(s_at, 1)
                if i >= 2:
                    q = i - 2
                    act.wait_ge(s_ctp, q + 1)
                    nc.scalar.activation(cur[:].rearrange("p t c -> p (t c)")[:, q * QT:(q + 1) * QT], ps[:, 4 + q % 2],
                                         ACT.Copy).then_inc(s_ct, 1)

            def hidden(m, c):
                act.wait_ge(s_w1, m + 1)
                if not (isinstance(m, int) and m < 2):
                    act.wait_ge(s_lo, m - 1)
                nc.scalar.activation(hid[:, c % 2], ps_h[:, c % 2], ACT.Gelu_apprx_tanh,
                                     bias=b1s[:, c:c + 1]).then_inc(s_gelu, 1)
                act.wait_ge(s_gelu, m + 1)
                nc.scalar.activation(hid_hi[:, c % RING], hid[:, c % 2], ACT.Copy).then_inc(s_hi, 1)

            def gate_tanh(n):
                act.wait_ge(s_arg, n + 1)
                nc.scalar.activation(tanh[:], arg[:], ACT.Tanh, scale=0.5).then_inc(s_tanh, 1)

            def round_(r, last):
                for k in range(RS):
                    if k == 11:
                        gate_tanh(2 * r + 1)
                    if k == 27 and not last:
                        gate_tanh(2 * r + 2)
                    if k + LAG < RS or not last:
                        hidden(RS * r + k + LAG, (k + LAG) % STEPS)

            gate_tanh(0)
            for m in range(LAG):
                hidden(m, m)
            with act.Fori(0, R - 1) as r:
                round_(r, False)
            round_(R - 1, True)

        @block.vector
        def _(dve):
            dve.wait_ge(s_ident, 1)
            nc.vector.tensor_reduce(head_mask[:], ident[:].rearrange("p (g j d) -> p j g d", g=G, j=J),
                                    mybir.AxisListType.XY, ALU.add).then_inc(s_mask, 1)
            dve.wait_ge(s_in_w, 96)
            nc.vector.tensor_copy(wqkv_hi[:], wqkv[:]).then_inc(s_wsplit, 1)
            dve.wait_ge(s_wsplit, 1)
            nc.vector.tensor_tensor(wqkv_lo[:], wqkv[:], wqkv_hi[:].bitcast(F32), ALU.subtract).then_inc(s_wsplit, 1)

            def moments(n, q, src):
                for i in range(q * QUAD, (q + 1) * QUAD):
                    last = nc.vector.bn_stats(stats[:, i], src[:, i])
                last.then_inc(s_stats, 1)
                dve.wait_ge(s_stats, n + 1)
                for i in range(q * QUAD, (q + 1) * QUAD):
                    last = nc.vector.bn_aggr(mean_var[:, i], stats[:, i])
                last.then_inc(s_mv, 1)

            def normalise(n, q, src):
                dve.wait_ge(s_rstd, n + 1)
                for i in range(QUAD):
                    b = q * QUAD + i
                    last = nc.vector.tensor_scalar(xn[:, q % 2, i], src[:, b], mean_var[:, b, 0:1], rstd[:, b:b + 1],
                                                   ALU.subtract, ALU.mult)
                last.then_inc(s_xn, 1)

            for i in range(NQ + 2):
                if i < NQ:
                    dve.wait_ge(s_in_x[i], 16)
                    moments(i, i, x_all)
                if 1 <= i <= NQ:
                    q = i - 1
                    if q >= 2:
                        dve.wait_ge(s_xtp, q - 1)
                    normalise(q, q, x_all)
                    dve.wait_ge(s_xth, q + 1)
                    nc.vector.tensor_tensor(xt_lo[:, q % 2], ps[:, q % 2], xt_hi[:, q % 2].bitcast(F32),
                                            ALU.subtract).then_inc(s_xtl, 1)
                if i >= 2:
                    q = i - 2
                    quad = slice(q * QUAD, (q + 1) * QUAD)
                    dve.wait_ge(s_kf, q + 1)
                    nc.vector.tensor_tensor(k_lo[:, quad, 0:KEYS], k_full[:, q % 2].rearrange("p (b s) -> p b s", s=KEYS),
                                            k_hi[:, quad, 0:KEYS].bitcast(F32), ALU.subtract).then_inc(s_kl, 1)
                    dve.wait_ge(s_vp, q + 1)
                    if q >= 2:
                        dve.wait_ge(s_v, q - 1)
                    nc.vector.tensor_tensor(v_full[:, q % 2].rearrange("p (b d) -> p b d", d=D),
                                            ps[0:KEYS, 4 + q % 2].rearrange("p (b d) -> p b d", d=D),
                                            bv[:, None, :].to_broadcast([KEYS, QUAD, D]), ALU.add).then_inc(s_vf, 1)
                    dve.wait_ge(s_qf, q + 1)
                    nc.vector.tensor_tensor(q_lo[:, quad], q_full[:, q % 2].rearrange("p (b s) -> p b s", s=S),
                                            q_hi[:, quad].bitcast(F32), ALU.subtract).then_inc(s_ql, 1)

            def softmax_shift(u, half):
                score = ps_score[:, 2 * half:2 * half + 2, 0:G * KPAD].rearrange("p g (j k) -> p g j k", k=KPAD)[:, :, :, 0:KEYS]
                dve.wait_ge(s_score, u + 1)
                nc.vector.tensor_reduce(top[:, half].rearrange("p (g j) -> p g j", j=J), score, AX_X, ALU.max).then_inc(s_top, 1)
                dve.wait_ge(s_top, u + 1)
                nc.vector.tensor_tensor(probs[:, half].rearrange("p (g j) k -> p g j k", j=J), score,
                                        top[:, half].rearrange("p (g j) -> p g j", j=J)[:, :, :, None].to_broadcast([P, 2, J, KEYS]),
                                        ALU.subtract).then_inc(s_sub, 1)

            def scale_values(b, slot):
                dve.wait_ge(s_pv, 2 * b + 2)
                nc.vector.tensor_reduce(summed[:], ps_o[:, slot].rearrange("p h c d -> p h d c"), AX_X, ALU.add).then_inc(s_osum, 1)
                dve.wait_ge(s_osum, b + 1)
                nc.vector.reciprocal(sum_inv[:], summed[:, :, DH]).then_inc(s_inv, 1)
                dve.wait_ge(s_inv, b + 1)
                at = attn[:, b] if isinstance(b, int) else attn[:, bass.ds(b, 1)].rearrange("p b d -> p (b d)")
                nc.vector.tensor_tensor(at.rearrange("p (h d) -> p h d", d=DH), summed[:, :, 0:DH],
                                        sum_inv[:, :, None].to_broadcast([P, H, DH]), ALU.mult).then_inc(s_attn, 1)

            def low_part(u, half):
                dve.wait_ge(s_pth, u + 1)
                nc.vector.scalar_tensor_tensor(probs_t[:, half, 1], ps_pt, PSCALE, probs_t[:, half, 0], ALU.mult,
                                               ALU.subtract).then_inc(s_pt, 1)

            def pair(p, first):
                for n in range(4):
                    if not (first and n == 0):
                        softmax_shift(4 * p + n, n % 2)
                        low_part(4 * p + n - 1, (n + 1) % 2)
                    if n % 2 == 1 and not (first and n == 1):
                        scale_values(2 * p - 1 + n // 2, (n // 2 + 1) % 2)

            softmax_shift(0, 0)
            pair(0, True)
            with dve.Fori(1, NB // 2) as p:
                pair(p, False)
            low_part(2 * NB - 1, 1)
            scale_values(NB - 1, 1)

            dve.wait_ge(s_xb, 1)
            cur_hi_all, cur_lo_all = (a.rearrange("p t c -> p (t c)") for a in (cur_hi, cur_lo))
            for i in range(NQ + 1):
                if i < NQ:
                    quad = slice(i * QUAD, (i + 1) * QUAD)
                    dve.wait_ge(s_op, i + 1)
                    nc.vector.tensor_tensor(x1[:, quad], ps[:, 2 + i % 2].rearrange("p (b d) -> p b d", d=D),
                                            xb[:, quad], ALU.add).then_inc(s_x1, 1)
                    dve.wait_ge(s_x1, i + 1)
                    moments(NQ + i, i, x1)
                if i >= 1:
                    q = i - 1
                    cols = slice(q * QT, (q + 1) * QT)
                    if q >= 2:
                        dve.wait_ge(s_ctp, q - 1)
                    normalise(NQ + q, q, x1)
                    dve.wait_ge(s_ct, q + 1)
                    nc.vector.tensor_copy(cur_hi_all[:, cols], ps[:, 4 + q % 2]).then_inc(s_chi3, 1)
                    dve.wait_ge(s_chi3, q + 1)
                    nc.vector.tensor_tensor(cur_lo_all[:, cols], ps[:, 4 + q % 2], cur_hi_all[:, cols].bitcast(F32),
                                            ALU.subtract).then_inc(s_cur3, 1)

            dve.sem_inc(s_stt, 2)

            GATE = 15

            def step(n, i, ins):
                ins.then_inc(s_gate, 1)
                dve.wait_ge(s_gate, GATE * n + i + 1)

            def gate_logits(n, r):
                dve.wait_ge(s_gl, n + 1)
                step(n, 0, nc.vector.tensor_tensor(
                    logit[:], ps[:, 6, 0:TG * E].rearrange("p (g e) -> p g e", e=E),
                    bgs[:, bass.ds(r * E, E)][:, None, :].to_broadcast([P, TG, E]), ALU.add))
                step(n, 1, nc.vector.tensor_tensor(hi2[:], logit[:, :, 0:2], logit[:, :, 2:4], ALU.max))
                step(n, 2, nc.vector.tensor_tensor(lo2[:], logit[:, :, 0:2], logit[:, :, 2:4], ALU.min))

            def gate_top2(n):
                step(n, 3, nc.vector.tensor_tensor(v12[:, 0], hi2[:, :, 0], hi2[:, :, 1], ALU.max))
                step(n, 4, nc.vector.tensor_tensor(v12[:, 1], hi2[:, :, 0], hi2[:, :, 1], ALU.min))
                step(n, 5, nc.vector.tensor_tensor(v12[:, 2], lo2[:, :, 0], lo2[:, :, 1], ALU.max))
                step(n, 6, nc.vector.tensor_tensor(v12[:, 3], v12[:, 1], v12[:, 2], ALU.max))

            def gate_args(n):
                step(n, 7, nc.vector.tensor_tensor(arg1[:], logit[:], v12[:, 0, :, None].to_broadcast([P, TG, E]), ALU.subtract))
                step(n, 8, nc.vector.tensor_tensor(arg[:], logit[:], v12[:, 3, :, None].to_broadcast([P, TG, E]), ALU.subtract))
                nc.vector.tensor_tensor(arg[:], arg[:], arg1[:], ALU.add).then_inc(s_arg, 1)

            def gate_beats(n):
                step(n, 9, nc.vector.tensor_tensor(
                    ge[:], logit[:, :, :, None].to_broadcast([P, TG, E, E]),
                    logit[:, :, None, :].to_broadcast([P, TG, E, E]), ALU.is_ge))
                step(n, 10, nc.vector.tensor_tensor(ge[:], ge[:], later[:], ALU.mult))
                step(n, 11, nc.vector.tensor_tensor(beat[:], ge[:], ge[:].rearrange("p g e j -> p g j e"), ALU.subtract))

            def gate_wins(n):
                step(n, 12, nc.vector.tensor_tensor(wins2[:], beat[:, :, :, 0:2], beat[:, :, :, 2:4], ALU.add))
                step(n, 13, nc.vector.tensor_tensor(wins[:], wins2[:, :, :, 0], wins2[:, :, :, 1], ALU.add))
                step(n, 14, nc.vector.tensor_tensor(wins[:], wins[:], wins_needed[:], ALU.is_ge))

            def gate_weights(n):
                dve.wait_ge(s_tanh, n + 1)
                nc.vector.tensor_scalar(tanh[:], tanh[:], 0.5, 0.5, ALU.mult, ALU.add).then_inc(s_tanh2, 1)
                dve.wait_ge(s_tanh2, n + 1)
                nc.vector.tensor_tensor(cw[:, 0:E * TG].rearrange("p (e g) -> p g e", e=E), tanh[:], wins[:],
                                        ALU.mult).then_inc(s_cw, 1)

            def gate_turned(n):
                dve.wait_ge(s_cwp, n + 1)
                nc.vector.tensor_copy(cw_t[:], ps[0:E * TG, 7, 0:P]).then_inc(s_cwt, 1)

            def hidden_low(m, c):
                dve.wait_ge(s_hi, m + 1)
                nc.vector.tensor_tensor(hid_lo[:, c % RING], hid[:, c % 2], hid_hi[:, c % RING].bitcast(F32),
                                        ALU.subtract).then_inc(s_lo, 1)

            def weigh(r, k):
                t, e, y = k // STEPS, k % STEPS // FC, 8 * r + k // FC
                dve.wait_ge(s_y, y + 1)
                dve.wait_ge(s_cwb, 2 * r + t + 1)
                dve.wait_ge(s_acc, y + 1)
                for h in range(2):
                    nc.vector.scalar_tensor_tensor(
                        y_w[:, (k // FC) % 2, h * HALF:(h + 1) * HALF], ps_y[:, h], b2s[:, e:e + 1],
                        cw_all[:, t, e, h * HALF:(h + 1) * HALF], ALU.add, ALU.mult).then_inc(s_stt, 1)

            def finish(n):
                dve.wait_ge(s_ftp, n + 1)
                nc.vector.tensor_tensor(xb[:, 4 * n:4 * n + 4], ps[:, 6 + n % 2].rearrange("p (b d) -> p b d", d=D),
                                        x1[:, 4 * n:4 * n + 4], ALU.add).then_inc(s_fin, 1)

            def round_(r, last):
                for k in range(RS):
                    for t, n, rn, k0 in ((1, 2 * r + 1, r, 0), (0, 2 * r + 2, r + 1, STEPS)):
                        if k0 and last:
                            continue
                        if k == k0 + 7:
                            gate_logits(n, rn)
                        if k == k0 + 8:
                            gate_top2(n)
                        if k == k0 + 9:
                            gate_args(n)
                        if k == k0 + 10:
                            gate_beats(n)
                        if k == k0 + 11:
                            gate_wins(n)
                        if k == k0 + 12:
                            gate_weights(n)
                        if k == k0 + 13:
                            gate_turned(n)
                    if k % FC == FC - 1:
                        weigh(r, k)
                    if last and k == STEPS + 4:
                        finish(0)
                        finish(1)
                    if k + LAG - 1 < RS or not last:
                        hidden_low(RS * r + k + LAG - 1, (k + LAG - 1) % STEPS)

            gate_logits(0, 0)
            gate_top2(0)
            gate_args(0)
            gate_beats(0)
            gate_wins(0)
            gate_weights(0)
            gate_turned(0)
            for m in range(LAG - 1):
                hidden_low(m, m)
            with dve.Fori(0, R - 1) as r:
                round_(r, False)
            round_(R - 1, True)
            finish(2)
            finish(3)

        @block.tensor
        def _(pe):
            def product(dst, w_hi, w_lo, a_hi, a_lo, start=True, stop=True):
                nc.tensor.matmul(dst, w_hi, a_lo, start=start, stop=False)
                nc.tensor.matmul(dst, w_lo, a_hi, start=False, stop=False)
                return nc.tensor.matmul(dst, w_hi, a_hi, start=False, stop=stop)

            pe.wait_ge(s_ident, 1)
            pe.wait_ge(s_wsplit, 2)
            pe.wait_ge(s_ctx, 1)
            for i in range(NQ + 1):
                if i < NQ:
                    quad = slice(i * QK, (i + 1) * QK)
                    if i >= 2:
                        pe.wait_ge(s_kf, i - 1)
                        pe.wait_ge(s_vf, i - 1)
                        pe.wait_ge(s_xtl, i - 1)
                    product(ps[:, 2 + i % 2, 0:QK], wqkv_hi[:, 1], wqkv_lo[:, 1], ctx_hi[:, quad], ctx_lo[:, quad])\
                        .then_inc(s_kp, 1)
                    for b in range(QUAD):
                        keys = slice((i * QUAD + b) * KEYS, (i * QUAD + b + 1) * KEYS)
                        last = product(ps[0:KEYS, 4 + i % 2, b * D:(b + 1) * D], ctx_hi[:, keys], ctx_lo[:, keys],
                                       wqkv_hi[:, 2], wqkv_lo[:, 2])
                    last.then_inc(s_vp, 1)
                    pe.wait_ge(s_xn, i + 1)
                    for b in range(QUAD):
                        last = nc.tensor.transpose(ps[:, i % 2, b * S:(b + 1) * S], xn[:, i % 2, b], ident[:])
                    last.then_inc(s_xtp, 1)
                if i >= 1:
                    q = i - 1
                    if q >= 2:
                        pe.wait_ge(s_qf, q - 1)
                    pe.wait_ge(s_xtl, q + 1)
                    product(ps[:, 6 + q % 2], wqkv_hi[:, 0], wqkv_lo[:, 0], xt_hi[:, q % 2], xt_lo[:, q % 2]).then_inc(s_qp, 1)

            def scores(u, b, half, slot):
                if half == 0:
                    pe.wait_ge(s_qk_slot, 4 * b + 4)
                if not (isinstance(u, int) and u < 2):
                    pe.wait_ge(s_sub, u - 1)
                for step, (qp, kp) in enumerate(((0, 1), (1, 0), (0, 0))):
                    for g in (2 * half, 2 * half + 1):
                        rows = slice(32 * g, 32 * g + 32)
                        last = nc.tensor.matmul(ps_score[:, g, 0:J * KPAD], q_slot[rows, slot, qp],
                                                k_slot[rows, slot, kp].rearrange("p j k -> p (j k)"),
                                                start=(step == 0), stop=(step == 2))
                last.then_inc(s_score, 1)

            def turn_probs(u, half):
                pe.wait_ge(s_exp, u + 1)
                if not (isinstance(u, int) and u < 1):
                    pe.wait_ge(s_pt, u)
                for i in range(HH):
                    last = nc.tensor.transpose(ps_pt[:, i], probs[:, half, i], ident[:])
                last.then_inc(s_ptp, 1)

            def values(u, b, half, slot):
                pe.wait_ge(s_pt, u + 1)
                if half == 0:
                    pe.wait_ge(s_v_slot, b + 1)
                    if not (isinstance(b, int) and b < 2):
                        pe.wait_ge(s_attn, b - 1)
                for i in range(HH):
                    h = half * HH + i
                    for part in range(2):
                        last = nc.tensor.matmul(ps_o[:, slot, h].rearrange("p c d -> p (c d)"), probs_t[:, half, part, i],
                                                v_slot[:, slot, h * 3 * (DH + 1):(h + 1) * 3 * (DH + 1)],
                                                start=(part == 0), stop=(part == 1))
                last.then_inc(s_pv, 1)

            def pair(p, last):
                for n in range(4):
                    u = 4 * p + n
                    if not (last and n >= 2):
                        scores(u + 2, 2 * p + n // 2 + 1, n % 2, (n // 2 + 1) % 2)
                    if not (last and n == 3):
                        turn_probs(u + 1, (n + 1) % 2)
                    values(u, 2 * p + n // 2, n % 2, n // 2)

            scores(0, 0, 0, 0)
            scores(1, 0, 1, 0)
            turn_probs(0, 0)
            pair(0, False)
            with pe.Fori(1, NB // 2 - 1) as p:
                pair(p, False)
            pair(NB // 2 - 1, True)

            pe.wait_ge(s_attn, NB)
            for i in range(NQ + 2):
                if i < NQ:
                    if i >= 2:
                        pe.wait_ge(s_at, i - 1)
                    for b in range(QUAD):
                        last = nc.tensor.transpose(ps[:, i % 2, b * S:(b + 1) * S], attn[:, i * QUAD + b], ident[:])
                    last.then_inc(s_atp, 1)
                if 1 <= i <= NQ:
                    q = i - 1
                    pe.wait_ge(s_at, q + 1)
                    if q >= 2:
                        pe.wait_ge(s_x1, q - 1)
                    for b in range(QUAD):
                        last = nc.tensor.matmul(ps[:, 2 + q % 2, b * D:(b + 1) * D], attn_t[:, q % 2, b * S:(b + 1) * S],
                                                wo[:], start=True, stop=True)
                    last.then_inc(s_op, 1)
                if i >= 2:
                    q = i - 2
                    pe.wait_ge(s_xn, NQ + q + 1)
                    if q >= 2:
                        pe.wait_ge(s_cur3, q - 1)
                    for b in range(QUAD):
                        last = nc.tensor.transpose(ps[:, 4 + q % 2, b * S:(b + 1) * S], xn[:, q % 2, b], ident[:])
                    last.then_inc(s_ctp, 1)

            def gate(t, n, r):
                pe.wait_ge(s_split, n + 1)
                for i in range(TG):
                    last = nc.tensor.matmul(ps[:, 6, i * E:(i + 1) * E], cur[:, t, i * P:(i + 1) * P],
                                            wgs[:, bass.ds(r * E, E)], start=True, stop=True)
                last.then_inc(s_gl, 1)

            def turn_gate(n):
                pe.wait_ge(s_cw, n + 1)
                nc.tensor.transpose(ps[:, 7, 0:P], cw[:], ident[:]).then_inc(s_cwp, 1)

            def first(m, c, t, n, wait_slot=True):
                if c == 0:
                    pe.wait_ge(s_split, n + 1)
                if wait_slot:
                    pe.wait_ge(s_gelu, m - 1)
                w = slice(c * P, (c + 1) * P)
                for h in range(2):
                    cols = slice(h * HALF, (h + 1) * HALF)
                    last = product(ps_h[:, c % 2, cols], w1_hi[:, w], w1_lo[:, w], cur_hi[:, t, cols], cur_lo[:, t, cols])
                last.then_inc(s_w1, 1)

            def second(r, k):
                c, y = k % STEPS, 8 * r + k // FC
                pe.wait_ge(s_lo, RS * r + k + 1)
                w = slice(c * P, (c + 1) * P)
                for h in range(2):
                    if c % FC == 0:
                        pe.wait_ge(s_stt, 2 * y + h + 1)
                    cols = slice(h * HALF, (h + 1) * HALF)
                    last = product(ps_y[:, h], w2_hi[:, w], w2_lo[:, w], hid_hi[:, c % RING, cols],
                                   hid_lo[:, c % RING, cols], c % FC == 0, c % FC == FC - 1)
                if c % FC == FC - 1:
                    last.then_inc(s_y, 1)

            def turn_back(n):
                t = n // 2
                pe.wait_ge(s_acc, 8 * (R - 1) + 4 * t + 6)
                for i in range(4):
                    c = (n % 2) * 4 + i
                    last = nc.tensor.transpose(ps[:, 6 + n % 2, i * P:(i + 1) * P], cur[:, t, c * P:(c + 1) * P], ident[:])
                last.then_inc(s_ftp, 1)

            def round_(r, last):
                for k in range(RS):
                    if k == 6:
                        gate(1, 2 * r + 1, r)
                    if k == 22 and not last:
                        gate(0, 2 * r + 2, r + 1)
                    if k == 13:
                        turn_gate(2 * r + 1)
                    if k == 29 and not last:
                        turn_gate(2 * r + 2)
                    if last and k == STEPS + 3:
                        turn_back(0)
                        turn_back(1)
                    second(r, k)
                    a = k + LAG
                    if a < RS:
                        first(RS * r + a, a % STEPS, a // STEPS, 2 * r + a // STEPS)
                    elif not last:
                        first(RS * r + a, a % STEPS, 0, 2 * r + 2)

            pe.wait_ge(s_fsplit, 2)
            gate(0, 0, 0)
            for m in range(LAG):
                first(m, m, 0, 0, wait_slot=(m >= 2))
            turn_gate(0)
            with pe.Fori(0, R - 1) as r:
                round_(r, False)
            round_(R - 1, True)
            turn_back(2)
            turn_back(3)


def kernel(x, ctx_1024, L0_xattn_wq, L0_xattn_bq, L0_xattn_wk, L0_xattn_bk, L0_xattn_wv, L0_xattn_bv, L0_xattn_wo,
           L0_xattn_bo, L0_ffn_Wg, L0_ffn_bg, L0_ffn_W1, L0_ffn_b1, L0_ffn_W2, L0_ffn_b2):
    import numpy as np
    import concourse.bacc as bacc
    from concourse.bass_utils import run_bass_kernel_spmd

    def laid(a):
        return np.ascontiguousarray(a)

    D = x.shape[-1]
    ctx = np.asarray(ctx_1024)
    arrays = {
        "x": laid(x),
        "ctx_t": laid(ctx.reshape(-1, D).T),
        "w_qkv": laid(np.stack([np.asarray(w).T for w in (L0_xattn_wq, L0_xattn_wk, L0_xattn_wv)], axis=1)),
        "w_o": laid(np.asarray(L0_xattn_wo).T),
        "b_qk": laid(np.stack([np.asarray(L0_xattn_bq), np.asarray(L0_xattn_bk)], axis=1)),
        "b_v": laid(L0_xattn_bv),
        "b_o": laid(L0_xattn_bo),
        "wg": laid(np.asarray(L0_ffn_Wg).transpose(1, 0, 2).reshape(D, -1)),
        "bg": laid(np.asarray(L0_ffn_bg).reshape(-1)),
        "w1": laid(L0_ffn_W1),
        "b1": laid(np.asarray(L0_ffn_b1).reshape(-1, 128).T),
        "w2": laid(np.asarray(L0_ffn_W2).reshape(-1, D)),
        "b2": laid(np.asarray(L0_ffn_b2).T),
    }
    nc = bacc.Bacc("TRN2", target_bir_lowering=False, num_devices=1)
    args = [nc.dram_tensor(f"in_{name}", a.shape, mybir.dt.from_np(a.dtype), kind="ExternalInput").ap()
            for name, a in arrays.items()]
    out = nc.dram_tensor("out_0", arrays["x"].shape, F32, kind="ExternalOutput").ap()
    xattn_moe(nc, *args, out)
    r = run_bass_kernel_spmd(nc, [{f"in_{name}": a for name, a in arrays.items()}], core_ids=[0])
    return r.results[0]["out_0"]
```

```python
from contextlib import ExitStack

import concourse.bass as bass
from concourse import mybir

F32 = mybir.dt.float32
F32R = mybir.dt.float32r
BF16 = mybir.dt.bfloat16
F16 = mybir.dt.float16
ALU = mybir.AluOpType
ACT = mybir.ActivationFunctionType
AX_X = mybir.AxisListType.X

P = 128
EPS = 1e-5


def xattn_moe(nc, x, ctx_t, w_qkv, w_o, b_qk, b_v, b_o, wg, bg, w1, b1, w2, b2, out):
    NB, S, D = x.shape
    KEYS = ctx_t.shape[1] // NB
    H, DH = 16, 8
    J = 4
    QUAD = 4
    QT, QK = QUAD * S, QUAD * KEYS
    NQ = NB // QUAD
    HH = H // 2
    E, R = b2.shape[1], wg.shape[1] // b2.shape[1]
    FC = b1.shape[1] // E
    T = NB * S // 2
    TG = T // P
    STEPS = E * FC
    RS = 2 * STEPS
    HALF = 512
    LAG = 3
    RING = 4
    SCALE = float(DH) ** -0.5
    PSCALE = 2.0 ** 14

    with ExitStack() as stack:
        def sb(name, shape, dt=F32):
            return stack.enter_context(nc.sbuf_tensor(name, shape, dt))

        def sem(name):
            return stack.enter_context(nc.semaphore(name))

        ident = sb("ident", [P, P])
        wqkv = sb("wqkv", [P, 3, D])
        wqkv_hi = sb("wqkv_hi", [P, 3, D], F32R)
        wqkv_lo = sb("wqkv_lo", [P, 3, D], F32R)
        wo = sb("wo", [P, D])
        bqk = sb("bqk", [P, 2])
        bv = sb("bv", [KEYS, D])
        bo = sb("bo", [P, D])
        head_mask = sb("head_mask", [P, HH])
        wgs = sb("wgs", [P, R * E])
        bgs = sb("bgs", [P, R * E])
        w1_hi = sb("w1_hi", [P, STEPS * P], F32R)
        w1_lo = sb("w1_lo", [P, STEPS * P], F32R)
        w2_hi = sb("w2_hi", [P, STEPS * P], F32R)
        w2_lo = sb("w2_lo", [P, STEPS * P], F32R)
        b1s = sb("b1s", [P, STEPS])
        b2s = sb("b2s", [P, E])
        minus_half = sb("minus_half", [P, NB])
        later = sb("later", [P, TG, E, E])
        wins_needed = sb("wins_needed", [P, TG, E])
        xb = sb("xb", [P, NB, D])
        ctx_all = sb("ctx_all", [P, NB * KEYS])
        stats = sb("stats", [P, NB, 6])
        mean_var = sb("mean_var", [P, NB, 2])
        var_eps = sb("var_eps", [P, NB])
        rstd = sb("rstd", [P, NB])
        xn = sb("xn", [P, 2, QUAD, D])
        attn_t = ctx_all[:, 0:2 * QT].rearrange("p (s c) -> p s c", s=2)
        q_slot = sb("q_slot", [P, 2, 2, S], F32R)
        v_slot = sb("v_slot", [P, 2, H * 3 * (DH + 1)], BF16)
        v_rest = sb("v_rest", [KEYS, D])
        top = sb("top", [P, 2, HH])
        shift = sb("shift", [P, 2, HH])
        summed = sb("summed", [P, H, DH + 1])
        sum_inv = sb("sum_inv", [P, H])
        x1 = sb("x1", [P, NB, D])
        cur = sb("cur", [P, 2, T])

        def parts_of(whole, *sizes):
            at = [sum(sizes[:i]) for i in range(len(sizes) + 1)]
            assert at[-1] <= whole.shape[1]
            return [whole[:, a:b] for a, b in zip(at, at[1:])]

        shared_r = sb("shared_r", [P, 2 * RING * T], F32R)
        q_hi, q_lo, k_hi, k_lo = parts_of(shared_r, NB * S, NB * S, NB * KEYS, NB * KEYS)
        q_hi, q_lo, k_hi, k_lo = (a.rearrange("p (b s) -> p b s", b=NB) for a in (q_hi, q_lo, k_hi, k_lo))
        q_parts = shared_r[:, 0:2 * NB * S].rearrange("p (c b s) -> p c b s", c=2, b=NB)
        hid_hi, hid_lo = (a.rearrange("p (s t) -> p s t", s=RING) for a in parts_of(shared_r, RING * T, RING * T))
        shared = sb("shared", [P, 2 * E * T])
        v_full, probs, probs_t = parts_of(shared, NB * D, H * KEYS, 2 * HH * S)
        v_full = v_full[0:KEYS].rearrange("p (b d) -> p b d", b=NB)
        probs = probs.rearrange("p (s h k) -> p s h k", s=2, h=HH)
        probs_t_rows = probs_t
        probs_t = probs_t.bitcast(F16).rearrange("p (s c b h t) -> p s c b h t", s=2, c=2, b=2, h=HH // 2)
        attn = cur[:].rearrange("p t (b d) -> p (t b) d", d=D)
        cw_all = shared[:].rearrange("p (t e c) -> p t e c", t=2, e=E)
        w12s = sb("w12s", [P, 2 * STEPS * P])
        w1s, w2s = parts_of(w12s, STEPS * P, STEPS * P)
        cw_row = w12s[0:1, 0:E * T]
        hid_or = sb("hid_or", [P, 2 * T])
        hid = hid_or[:].rearrange("p (s t) -> p s t", s=2)
        q_full, k_full = parts_of(hid_or, 2 * QT, 2 * QK)
        q_full, k_full = q_full.rearrange("p (s c) -> p s c", s=2), k_full.rearrange("p (s c) -> p s c", s=2)
        curs_r = sb("curs_r", [P, 4 * T], F32R)
        cur_hi, cur_lo = (a.rearrange("p (t c) -> p t c", t=2) for a in parts_of(curs_r, 2 * T, 2 * T))
        xt_hi, xt_lo = (a.rearrange("p (s c) -> p s c", s=2) for a in parts_of(curs_r, 2 * QT, 2 * QT))
        k_slot = [curs_r[:, at:at + 4 * J * KEYS].rearrange("p (c g j k) -> p c g j k", c=2, g=2, j=J) for at in (2 * T, 0)]
        ctx_r = sb("ctx_r", [P, 2 * NB * KEYS], F32R)
        ctx_hi, ctx_lo = parts_of(ctx_r, NB * KEYS, NB * KEYS)
        x_or_y = sb("x_or_y", [P, NB * D])
        x_all = x_or_y[:].rearrange("p (b d) -> p b d", b=NB)
        y_w = x_or_y[:].rearrange("p (s t) -> p s t", s=2)

        ps = stack.enter_context(nc.psum_tensor("ps", [P, 8, 512], F32))
        ps_score = ps[:, 0:4]
        ps_pt = ps[0:KEYS, 4:6].rearrange("p b (h s) -> p b h s", s=S)
        ps_o = ps[:, 6:8, 0:H * 3 * (DH + 1)].rearrange("p b (h c d) -> p b h c d", c=3, d=DH + 1)

        s_in_x = [sem(f"s_in_x{q}") for q in range(NQ)]
        s_in_w, s_in_o, s_in_f, s_in_w2 = sem("s_in_w"), sem("s_in_o"), sem("s_in_f"), sem("s_in_w2")
        s_ident, s_pool, s_mask, s_wsplit, s_fsplit = sem("s_ident"), sem("s_pool"), sem("s_mask"), sem("s_wsplit"), sem("s_fsplit")
        s_whi, s_unread, s_xb, s_nought = sem("s_whi"), sem("s_unread"), sem("s_xb"), sem("s_nought")
        s_stats, s_mv, s_ve, s_rstd, s_xn = sem("s_stats"), sem("s_mv"), sem("s_ve"), sem("s_rstd"), sem("s_xn")
        s_xtp, s_xth, s_xtl = sem("s_xtp"), sem("s_xth"), sem("s_xtl")
        s_qp, s_qf, s_ql = sem("s_qp"), sem("s_qf"), sem("s_ql")
        s_ctxh, s_ctx, s_kp, s_kf, s_kl = sem("s_ctxh"), sem("s_ctx"), sem("s_kp"), sem("s_kf"), sem("s_kl")
        s_vp, s_vf, s_vsplit = sem("s_vp"), sem("s_vf"), sem("s_vsplit")
        s_q_slot, s_k_slot, s_v_slot = sem("s_q_slot"), sem("s_k_slot"), sem("s_v_slot")
        s_score, s_top, s_shift, s_exp = sem("s_score"), sem("s_top"), sem("s_shift"), sem("s_exp")
        s_ptp, s_pth, s_pt, s_osum = sem("s_ptp"), sem("s_pth"), sem("s_pt"), sem("s_osum")
        s_pv, s_inv, s_attn = sem("s_pv"), sem("s_inv"), sem("s_attn")
        s_atp, s_at, s_op, s_x1 = sem("s_atp"), sem("s_at"), sem("s_op"), sem("s_x1")
        s_ctp, s_ct, s_cur3 = sem("s_ctp"), sem("s_ct"), sem("s_cur3")
        s_w1, s_gelu, s_hi, s_lo = sem("s_w1"), sem("s_gelu"), sem("s_hi"), sem("s_lo")
        s_y, s_stt, s_acc, s_chi, s_split = sem("s_y"), sem("s_stt"), sem("s_acc"), sem("s_chi"), sem("s_split")
        s_tanh2 = sem("s_tanh2")
        s_gl, s_gate, s_arg, s_tanh, s_cw = sem("s_gl"), sem("s_gate"), sem("s_arg"), sem("s_tanh"), sem("s_cw")
        s_cwp, s_cwt, s_row, s_cwb = sem("s_cwp"), sem("s_cwt"), sem("s_row"), sem("s_cwb")
        s_ftp, s_fin, s_out = sem("s_ftp"), sem("s_fin"), sem("s_out")

        logit = sb("logit", [P, TG, E])
        hi2 = sb("hi2", [P, TG, 2])
        lo2 = sb("lo2", [P, TG, 2])
        v12 = sb("v12", [P, 4, TG])
        ge = sb("ge", [P, TG, E, E])
        beat = sb("beat", [P, TG, E, E])
        wins2 = sb("wins2", [P, TG, E, 2])
        wins = sb("wins", [P, TG, E])
        arg1 = sb("arg1", [P, TG, E])
        arg = sb("arg", [P, TG, E])
        tanh = sb("tanh", [P, TG, E])
        cw = sb("cw", [P, P])
        cw_t = sb("cw_t", [E * TG, P])
        ps_h = ps[:, 0:4].rearrange("p (s b) c -> p s (b c)", s=2)
        ps_y = ps[:, 4:6]
        ps_ct = [ps[:, bank] for bank in (6, 7, 4, 5)]

        block = stack.enter_context(nc.Block())

        def wait_apart(eng, semaphore, value):
            eng.wait_ge(semaphore, value)
            eng.sem_inc(s_unread, 1)

        @block.sync
        def _(sp):
            for dst, src in ((wqkv[:], w_qkv), (ctx_all[:], ctx_t), (bqk[:], b_qk),
                             (bv[:], b_v[None, :].to_broadcast([KEYS, D]))):
                sp.dma_start(dst, src).then_inc(s_in_w, 16)
            for q in range(NQ):
                quad = slice(q * QUAD, (q + 1) * QUAD)
                sp.dma_start(x_all[:, quad], x.rearrange("b s d -> s b d")[:, quad]).then_inc(s_in_x[q], 16)
            for dst, src in ((wo[:], w_o), (bo[:], b_o[None, :].to_broadcast([P, D]))):
                sp.dma_start(dst, src).then_inc(s_in_o, 16)
            sp.dma_start(w1s.rearrange("p (e f) -> p e f", e=E), w1.rearrange("e h f -> h e f")).then_inc(s_in_f, 16)
            for dst, src in ((wgs[:], wg), (bgs[:], bg[None, :].to_broadcast([P, R * E])), (b1s[:], b1), (b2s[:], b2)):
                sp.dma_start(dst, src).then_inc(s_in_f, 16)
            sp.dma_start(w2s.rearrange("p (c h) -> p c h", h=D), w2.rearrange("(c p) h -> p c h", p=P)).then_inc(s_in_w2, 16)

            def row(n):
                sp.wait_ge(s_cwt, n + 1)
                sp.dma_start(cw_row, cw_t[:]).then_inc(s_row, 16)

            row(0)
            with sp.Fori(0, R - 1) as r:
                row(2 * r + 1)
                row(2 * r + 2)
            row(2 * R - 1)
            for t in range(2):
                for i in range(2):
                    n = 2 * t + i
                    sp.wait_ge(s_fin, n + 1)
                    sp.dma_start(out.rearrange("b s d -> s b d")[:, 4 * n:4 * n + 4],
                                 xb[:, 4 * n:4 * n + 4]).then_inc(s_out, 16)
            sp.wait_ge(s_out, 64)

        @block.gpsimd
        def _(pool):
            nc.gpsimd.memset(ident[:], 0.0).then_inc(s_pool, 1)
            nc.gpsimd.memset(later[:], 0.0).then_inc(s_pool, 1)
            pool.wait_ge(s_pool, 2)
            nc.gpsimd.affine_select(out=ident[:], in_=ident[:], compare_op=ALU.not_equal, fill=1.0, base=0,
                                    pattern=[[-1, P]], channel_multiplier=1).then_inc(s_ident, 1)
            v_slots = v_slot[:].rearrange("p s (h c d) -> p s h c d", h=H, c=3)
            nc.gpsimd.memset(v_slot[:], 0.0).then_inc(s_pool, 1)
            pool.wait_ge(s_pool, 3)
            nc.gpsimd.memset(v_slots[0:KEYS, :, :, 0, DH], 1.0).then_inc(s_pool, 1)
            nc.gpsimd.memset(probs_t_rows, 0.0).then_inc(s_nought, 1)
            nc.gpsimd.memset(minus_half[:], -0.5).then_inc(s_pool, 1)
            nc.gpsimd.memset(cw[:], 0.0).then_inc(s_pool, 1)
            for e in range(E):
                nc.gpsimd.memset(wins_needed[:, :, e], 2.0 - e).then_inc(s_pool, 1)
                if e < E - 1:
                    nc.gpsimd.memset(later[:, :, e, e + 1:E], 1.0).then_inc(s_pool, 1)

            def inverse_deviation(n, q):
                quad = slice(q * QUAD, (q + 1) * QUAD)
                pool.wait_ge(s_mv, n + 1)
                nc.gpsimd.tensor_scalar(var_eps[:, quad], mean_var[:, quad, 1], EPS, 1.0, ALU.add, ALU.mult).then_inc(s_ve, 1)
                pool.wait_ge(s_ve, n + 1)
                nc.gpsimd.tensor_tensor(rstd[:, quad], var_eps[:, quad], minus_half[:, quad], ALU.pow).then_inc(s_rstd, 1)

            for q in range(NQ):
                inverse_deviation(q, q)

            def key_slot(b, slot):
                one = bass.ds(b, 1)
                for part, k in ((0, k_hi), (1, k_lo)):
                    nc.gpsimd.tensor_tensor(k_slot[slot][:, part].rearrange("p g j k -> p (g j) k"),
                                            k[:, one].bitcast(F32).to_broadcast([P, HH, KEYS]),
                                            head_mask[:, :, None].to_broadcast([P, HH, KEYS]), ALU.mult).then_inc(s_k_slot, 1)

            def value_slot(b, slot):
                one = v_full[:, bass.ds(b, 1)].rearrange("p b (h d) -> p (b h) d", h=H)
                rest = v_rest[:].rearrange("p (h d) -> p h d", h=H)
                part = [v_slots[0:KEYS, slot, :, c, 0:DH] for c in range(3)]
                nc.gpsimd.tensor_copy(part[0], one).then_inc(s_vsplit, 1)
                wait_apart(pool, s_vsplit, 3 * b + 1)
                nc.gpsimd.tensor_tensor(rest, one, part[0], ALU.subtract).then_inc(s_vsplit, 1)
                wait_apart(pool, s_vsplit, 3 * b + 2)
                nc.gpsimd.tensor_copy(part[1], rest).then_inc(s_vsplit, 1)
                wait_apart(pool, s_vsplit, 3 * b + 3)
                nc.gpsimd.tensor_tensor(part[2], rest, part[1], ALU.subtract).then_inc(s_v_slot, 1)

            def biased(b):
                one = bass.ds(b, 1)
                nc.gpsimd.tensor_tensor(xb[:, one], x_all[:, one], bo[:, None, :], ALU.add).then_inc(s_xb, 1)

            def weights_low(n):
                lo, hi, full = ((w1_lo, w1_hi, w1s), (w2_lo, w2_hi, w2s))[n]
                pool.wait_ge(s_whi, n + 1)
                nc.gpsimd.tensor_tensor(lo[:], full, hi[:].bitcast(F32), ALU.subtract).then_inc(s_fsplit, 1)

            weights_low(0)
            pool.wait_ge(s_mask, 1)
            pool.wait_ge(s_in_o, 32)
            for b in range(2):
                if b == 0:
                    pool.wait_ge(s_kl, 1)
                else:
                    pool.wait_ge(s_qp, NQ)
                key_slot(b, b)
                pool.wait_ge(s_vf, 1)
                value_slot(b, b)
                biased(b)
            weights_low(1)
            pool.wait_ge(s_kl, NQ)
            pool.wait_ge(s_vf, NQ)

            def pair(p, first, last):
                for i in range(2):
                    if not (last and i == 1) and not (first and i == 0):
                        wait_apart(pool, s_score, 4 * p + 2 * i)
                        key_slot(2 * p + i + 1, (i + 1) % 2)
                    if not first:
                        wait_apart(pool, s_pv, 4 * p + 2 * i - 2)
                        value_slot(2 * p + i, i)
                        biased(2 * p + i)

            pair(0, True, False)
            with pool.Fori(1, NB // 2 - 1) as p:
                pair(p, False, False)
            pair(NB // 2 - 1, False, True)

            for q in range(NQ):
                inverse_deviation(NQ + q, q)
                if q >= 2:
                    pool.wait_ge(s_cur3, (q - 1) * NQ // 2)
                    pool.sem_inc(s_split, 1)
            pool.sem_inc(s_acc, 2)

            def spread(t, n):
                wait_apart(pool, s_row, 16 * (n + 1))
                nc.gpsimd.partition_broadcast(cw_all[:, t].rearrange("p e t -> p (e t)"), cw_row, P)\
                    .then_inc(s_cwb, 1)

            def accumulate(r, k):
                t, y = k // STEPS, 8 * r + k // FC
                pool.wait_ge(s_stt, 2 * y + 4)
                pool.wait_ge(s_acc, y + 2)
                nc.gpsimd.tensor_tensor(cur[:, t], cur[:, t], y_w[:, (k // FC) % 2], ALU.add).then_inc(s_acc, 1)

            def split(r, t):
                n = 2 * r + t
                wait_apart(pool, s_acc, 8 * r + 4 * t + 6)
                nc.gpsimd.tensor_copy(cur_hi[:, t], cur[:, t]).then_inc(s_chi, 1)
                pool.wait_ge(s_chi, n + 1)
                nc.gpsimd.tensor_tensor(cur_lo[:, t], cur[:, t], cur_hi[:, t].bitcast(F32), ALU.subtract)\
                    .then_inc(s_split, 1)

            def round_(r, last):
                for k in range(FC - 1, RS, FC):
                    if k == 15:
                        spread(1, 2 * r + 1)
                    if k == 31 and not last:
                        spread(0, 2 * r + 2)
                    accumulate(r, k)
                    if k % STEPS == STEPS - 1 and not last:
                        split(r, k // STEPS)

            spread(0, 0)
            with pool.Fori(0, R - 1) as r:
                round_(r, False)
            round_(R - 1, True)

        @block.scalar
        def _(act):
            def key_high(q):
                act.wait_ge(s_kp, q + 1)
                if q >= 2:
                    act.wait_ge(s_kl, q - 1)
                nc.scalar.activation(k_full[:, q % 2], ps[:, 2 + q % 2, 0:QK], ACT.Identity, bias=bqk[:, 1:2])
                nc.scalar.activation(k_hi[:, q * QUAD:(q + 1) * QUAD, 0:KEYS],
                                     ps[:, 2 + q % 2, 0:QK].rearrange("p (b s) -> p b s", s=KEYS),
                                     ACT.Identity, bias=bqk[:, 1:2]).then_inc(s_kf, 1)

            def token_high(q):
                act.wait_ge(s_xtp, q + 1)
                if q >= 2:
                    act.wait_ge(s_qp, q - 1)
                nc.scalar.activation(xt_hi[:, q % 2], ps[:, q % 2], ACT.Copy).then_inc(s_xth, 1)

            def query_high(q):
                act.wait_ge(s_qp, q + 1)
                if q >= 2:
                    act.wait_ge(s_ql, q - 1)
                nc.scalar.activation(q_full[:, q % 2], ps[:, 6 + q % 2], ACT.Identity, bias=bqk[:, 0:1])
                nc.scalar.activation(q_hi[:, q * QUAD:(q + 1) * QUAD], ps[:, 6 + q % 2].rearrange("p (b s) -> p b s", s=S),
                                     ACT.Identity, bias=bqk[:, 0:1]).then_inc(s_qf, 1)

            act.wait_ge(s_in_w, 64)
            for q in range(NQ):
                quad = slice(q * QK, (q + 1) * QK)
                nc.scalar.activation(ctx_hi[:, quad], ctx_all[:, quad], ACT.Copy).then_inc(s_ctxh, 1)
            key_high(0)
            key_high(1)
            for i in range(NQ + 1):
                if i < NQ:
                    token_high(i)
                if i == 0:
                    act.wait_ge(s_in_f, 80)
                    nc.scalar.activation(w1_hi[:], w1s, ACT.Copy).then_inc(s_whi, 1)
                    act.wait_ge(s_in_w2, 16)
                    nc.scalar.activation(w2_hi[:], w2s, ACT.Copy).then_inc(s_whi, 1)
                if i >= 1:
                    query_high(i - 1)
                if i + 2 < NQ:
                    key_high(i + 2)

            def exp(u, half):
                act.wait_ge(s_shift, u + 1)
                for i in range(HH):
                    last = nc.scalar.activation(probs[:, half, i], ps_score[:, 2 * half + i // J, i % J * KEYS:(i % J + 1) * KEYS],
                                                ACT.Exp, bias=shift[:, half, i:i + 1], scale=SCALE)
                last.then_inc(s_exp, 1)

            def query_slot(b, slot):
                if not (isinstance(b, int) and b < 2):
                    wait_apart(act, s_score, 2 * b - 2)
                nc.scalar.activation(q_slot[:, slot], q_parts[:, :, bass.ds(b, 1)].bitcast(F32).rearrange("p c b s -> p c (b s)"),
                                     ACT.Copy).then_inc(s_q_slot, 1)

            def keep_probs_t(u, half):
                for bank in range(2):
                    act.wait_ge(s_ptp, 2 * u + bank + 1)
                    if bank == 0 and not (isinstance(u, int) and u < 2):
                        act.wait_ge(s_pv, u - 1)
                    nc.scalar.activation(probs_t[0:KEYS, half, 0, bank], ps_pt[:, bank], ACT.Copy, scale=PSCALE).then_inc(s_pth, 1)

            def keep_attn_t(q):
                act.wait_ge(s_atp, q + 1)
                if q >= 2:
                    act.wait_ge(s_op, q - 1)
                nc.scalar.activation(attn_t[:, q % 2], ps[:, q % 2], ACT.Copy).then_inc(s_at, 1)

            def pair(p, last):
                for n in range(4):
                    u = 4 * p + n
                    if not (last and n >= 2):
                        exp(u + 2, n % 2)
                    if not (last and n == 3):
                        keep_probs_t(u + 1, (n + 1) % 2)
                    if last and n == 1:
                        keep_attn_t(0)
                        keep_attn_t(1)
                    if n % 2 == 0 and not last:
                        query_slot(2 * p + 2 + n // 2, n // 2)

            act.wait_ge(s_ql, 1)
            query_slot(0, 0)
            query_slot(1, 1)
            act.wait_ge(s_ql, NQ)
            act.wait_ge(s_nought, 1)
            exp(0, 0)
            exp(1, 1)
            keep_probs_t(0, 0)
            pair(0, False)
            with act.Fori(1, NB // 2 - 1) as p:
                pair(p, False)
            pair(NB // 2 - 1, True)

            def keep_cur(q):
                act.wait_ge(s_ctp, q + 1)
                for tokens in (cur[:], cur_hi):
                    nc.scalar.activation(tokens.rearrange("p t c -> p (t c)")[:, q * QT:(q + 1) * QT], ps_ct[q],
                                         ACT.Copy).then_inc(s_ct, 1)

            for q in range(2, NQ):
                keep_attn_t(q)
            keep_cur(0)
            keep_cur(1)

            def hidden(m, c):
                act.wait_ge(s_w1, m + 1)
                if not (isinstance(m, int) and m < 2):
                    act.wait_ge(s_lo, m - 1)
                nc.scalar.activation(hid[:, c % 2], ps_h[:, c % 2], ACT.Gelu_apprx_tanh,
                                     bias=b1s[:, c:c + 1]).then_inc(s_gelu, 1)
                act.wait_ge(s_gelu, m + 1)
                nc.scalar.activation(hid_hi[:, c % RING], hid[:, c % 2], ACT.Copy).then_inc(s_hi, 1)

            def gate_tanh(n):
                act.wait_ge(s_arg, n + 1)
                nc.scalar.activation(tanh[:], arg[:], ACT.Tanh, scale=0.5).then_inc(s_tanh, 1)

            def round_(r, last):
                for k in range(RS):
                    if k == 11:
                        gate_tanh(2 * r + 1)
                    if k == 27 and not last:
                        gate_tanh(2 * r + 2)
                    if k + LAG < RS or not last:
                        hidden(RS * r + k + LAG, (k + LAG) % STEPS)

            hidden(0, 0)
            gate_tanh(0)
            keep_cur(2)
            keep_cur(3)
            hidden(1, 1)
            hidden(2, 2)
            with act.Fori(0, R - 1) as r:
                round_(r, False)
            round_(R - 1, True)

        @block.vector
        def _(dve):
            dve.wait_ge(s_ident, 1)
            nc.vector.tensor_reduce(head_mask[:], ident[:].rearrange("p (u j d) -> p j u d", u=2, j=HH),
                                    mybir.AxisListType.XY, ALU.add).then_inc(s_mask, 1)
            dve.wait_ge(s_in_w, 64)
            nc.vector.tensor_copy(wqkv_hi[:], wqkv[:]).then_inc(s_wsplit, 1)
            dve.wait_ge(s_wsplit, 1)
            nc.vector.tensor_tensor(wqkv_lo[:], wqkv[:], wqkv_hi[:].bitcast(F32), ALU.subtract).then_inc(s_wsplit, 1)

            def context_low(q):
                quad = slice(q * QK, (q + 1) * QK)
                dve.wait_ge(s_ctxh, q + 1)
                nc.vector.tensor_tensor(ctx_lo[:, quad], ctx_all[:, quad], ctx_hi[:, quad].bitcast(F32),
                                        ALU.subtract).then_inc(s_ctx, 1)

            def moments(n, q, src):
                for i in range(q * QUAD, (q + 1) * QUAD):
                    last = nc.vector.bn_stats(stats[:, i], src[:, i])
                last.then_inc(s_stats, 1)
                dve.wait_ge(s_stats, n + 1)
                for i in range(q * QUAD, (q + 1) * QUAD):
                    last = nc.vector.bn_aggr(mean_var[:, i], stats[:, i])
                last.then_inc(s_mv, 1)

            def normalise(n, q, src):
                dve.wait_ge(s_rstd, n + 1)
                for i in range(QUAD):
                    b = q * QUAD + i
                    last = nc.vector.tensor_scalar(xn[:, q % 2, i], src[:, b], mean_var[:, b, 0:1], rstd[:, b:b + 1],
                                                   ALU.subtract, ALU.mult)
                last.then_inc(s_xn, 1)

            def token_low(q):
                dve.wait_ge(s_xth, q + 1)
                nc.vector.tensor_tensor(xt_lo[:, q % 2], ps[:, q % 2], xt_hi[:, q % 2].bitcast(F32),
                                        ALU.subtract).then_inc(s_xtl, 1)

            def key_low(q):
                quad = slice(q * QUAD, (q + 1) * QUAD)
                dve.wait_ge(s_kf, q + 1)
                nc.vector.tensor_tensor(k_lo[:, quad, 0:KEYS], k_full[:, q % 2].rearrange("p (b s) -> p b s", s=KEYS),
                                        k_hi[:, quad, 0:KEYS].bitcast(F32), ALU.subtract).then_inc(s_kl, 1)

            def value(q):
                dve.wait_ge(s_vp, q + 1)
                nc.vector.tensor_tensor(v_full[:, q * QUAD:(q + 1) * QUAD], ps[0:KEYS, 4 + q % 2].rearrange("p (b d) -> p b d", d=D),
                                        bv[:, None, :].to_broadcast([KEYS, QUAD, D]), ALU.add).then_inc(s_vf, 1)

            def query_low(q):
                quad = slice(q * QUAD, (q + 1) * QUAD)
                dve.wait_ge(s_qf, q + 1)
                nc.vector.tensor_tensor(q_lo[:, quad], q_full[:, q % 2].rearrange("p (b s) -> p b s", s=S),
                                        q_hi[:, quad].bitcast(F32), ALU.subtract).then_inc(s_ql, 1)

            def token_moments(q):
                dve.wait_ge(s_in_x[q], 16)
                moments(q, q, x_all)

            context_low(0)
            token_moments(0)
            context_low(1)
            token_moments(1)
            normalise(0, 0, x_all)
            value(0)
            context_low(2)
            context_low(3)
            token_moments(2)
            normalise(1, 1, x_all)
            for i in range(NQ + 1):
                if i < NQ:
                    token_low(i)
                if i + 1 < NQ:
                    value(i + 1)
                if i < NQ:
                    key_low(i)
                if i + 3 < NQ:
                    token_moments(i + 3)
                if i + 2 < NQ:
                    dve.wait_ge(s_xtp, i + 1)
                    normalise(i + 2, i + 2, x_all)
                if i >= 1:
                    query_low(i - 1)

            def softmax_shift(u, half):
                score = ps_score[:, 2 * half:2 * half + 2, 0:J * KEYS].rearrange("p g (j k) -> p g j k", k=KEYS)
                dve.wait_ge(s_score, u + 1)
                nc.vector.tensor_reduce(top[:, half].rearrange("p (g j) -> p g j", j=J), score, AX_X, ALU.max).then_inc(s_top, 1)
                dve.wait_ge(s_top, u + 1)
                nc.vector.tensor_scalar(shift[:, half], top[:, half], -SCALE, 0.0, ALU.mult, ALU.add).then_inc(s_shift, 1)

            def scale_values(b, slot):
                dve.wait_ge(s_pv, 2 * b + 2)
                if not (isinstance(b, int) and b < 1):
                    dve.wait_ge(s_attn, b)
                nc.vector.tensor_reduce(summed[:], ps_o[:, slot].rearrange("p h c d -> p h d c"), AX_X, ALU.add).then_inc(s_osum, 1)
                dve.wait_ge(s_osum, b + 1)
                nc.vector.reciprocal(sum_inv[:], summed[:, :, DH]).then_inc(s_inv, 1)
                dve.wait_ge(s_inv, b + 1)
                at = attn[:, b] if isinstance(b, int) else attn[:, bass.ds(b, 1)].rearrange("p b d -> p (b d)")
                nc.vector.tensor_tensor(at.rearrange("p (h d) -> p h d", d=DH), summed[:, :, 0:DH],
                                        sum_inv[:, :, None].to_broadcast([P, H, DH]), ALU.mult).then_inc(s_attn, 1)

            def low_part(u, half):
                for bank in range(2):
                    dve.wait_ge(s_pth, 2 * u + bank + 1)
                    nc.vector.scalar_tensor_tensor(probs_t[0:KEYS, half, 1, bank], ps_pt[:, bank], PSCALE,
                                                   probs_t[0:KEYS, half, 0, bank], ALU.mult, ALU.subtract).then_inc(s_pt, 1)

            def pair(p, first, last):
                for n in range(4):
                    u = 4 * p + n
                    if not (last and n >= 1):
                        softmax_shift(u + 3, (n + 1) % 2)
                    if not (last and n == 3):
                        low_part(u + 1, (n + 1) % 2)
                    if n % 2 == 0 and not (first and n == 0):
                        scale_values(2 * p - 1 + n // 2, (n // 2 + 1) % 2)

            softmax_shift(0, 0)
            softmax_shift(1, 1)
            softmax_shift(2, 0)
            low_part(0, 0)
            pair(0, True, False)
            with dve.Fori(1, NB // 2 - 1) as p:
                pair(p, False, False)
            pair(NB // 2 - 1, False, True)

            dve.wait_ge(s_xb, NB)

            def residual(q):
                quad = slice(q * QUAD, (q + 1) * QUAD)
                dve.wait_ge(s_op, q + 1)
                nc.vector.tensor_tensor(x1[:, quad], ps[:, 2 + q % 2].rearrange("p (b d) -> p b d", d=D),
                                        xb[:, quad], ALU.add).then_inc(s_x1, 1)
                dve.wait_ge(s_x1, q + 1)
                moments(NQ + q, q, x1)

            def normalise_x1(q):
                if q >= 2:
                    dve.wait_ge(s_ctp, q - 1)
                normalise(NQ + q, q, x1)

            def cur_low(q):
                cols = slice(q * QT, (q + 1) * QT)
                dve.wait_ge(s_ct, 2 * q + 2)
                nc.vector.tensor_tensor(cur_lo.rearrange("p t c -> p (t c)")[:, cols], ps_ct[q],
                                        cur_hi.rearrange("p t c -> p (t c)")[:, cols].bitcast(F32),
                                        ALU.subtract).then_inc(s_cur3, 1)

            residual(0)
            scale_values(NB - 1, 1)
            residual(1)
            normalise_x1(0)
            normalise_x1(1)
            cur_low(0)
            residual(2)
            cur_low(1)
            residual(3)
            normalise_x1(2)

            GATE = 15

            def step(n, i, ins):
                ins.then_inc(s_gate, 1)
                dve.wait_ge(s_gate, GATE * n + i + 1)

            def gate_logits(n, r):
                dve.wait_ge(s_gl, n + 1)
                step(n, 0, nc.vector.tensor_tensor(
                    logit[:], ps[:, 6, 0:TG * E].rearrange("p (g e) -> p g e", e=E),
                    bgs[:, bass.ds(r * E, E)][:, None, :].to_broadcast([P, TG, E]), ALU.add))
                step(n, 1, nc.vector.tensor_tensor(hi2[:], logit[:, :, 0:2], logit[:, :, 2:4], ALU.max))
                step(n, 2, nc.vector.tensor_tensor(lo2[:], logit[:, :, 0:2], logit[:, :, 2:4], ALU.min))

            def gate_top2(n):
                step(n, 3, nc.vector.tensor_tensor(v12[:, 0], hi2[:, :, 0], hi2[:, :, 1], ALU.max))
                step(n, 4, nc.vector.tensor_tensor(v12[:, 1], hi2[:, :, 0], hi2[:, :, 1], ALU.min))
                step(n, 5, nc.vector.tensor_tensor(v12[:, 2], lo2[:, :, 0], lo2[:, :, 1], ALU.max))
                step(n, 6, nc.vector.tensor_tensor(v12[:, 3], v12[:, 1], v12[:, 2], ALU.max))

            def gate_args(n):
                step(n, 7, nc.vector.tensor_tensor(arg1[:], logit[:], v12[:, 0, :, None].to_broadcast([P, TG, E]), ALU.subtract))
                step(n, 8, nc.vector.tensor_tensor(arg[:], logit[:], v12[:, 3, :, None].to_broadcast([P, TG, E]), ALU.subtract))
                nc.vector.tensor_tensor(arg[:], arg[:], arg1[:], ALU.add).then_inc(s_arg, 1)

            def gate_beats(n):
                step(n, 9, nc.vector.tensor_tensor(
                    ge[:], logit[:, :, :, None].to_broadcast([P, TG, E, E]),
                    logit[:, :, None, :].to_broadcast([P, TG, E, E]), ALU.is_ge))
                step(n, 10, nc.vector.tensor_tensor(ge[:], ge[:], later[:], ALU.mult))
                step(n, 11, nc.vector.tensor_tensor(beat[:], ge[:], ge[:].rearrange("p g e j -> p g j e"), ALU.subtract))

            def gate_wins(n):
                step(n, 12, nc.vector.tensor_tensor(wins2[:], beat[:, :, :, 0:2], beat[:, :, :, 2:4], ALU.add))
                step(n, 13, nc.vector.tensor_tensor(wins[:], wins2[:, :, :, 0], wins2[:, :, :, 1], ALU.add))
                step(n, 14, nc.vector.tensor_tensor(wins[:], wins[:], wins_needed[:], ALU.is_ge))

            def gate_weights(n):
                dve.wait_ge(s_tanh, n + 1)
                nc.vector.tensor_scalar(tanh[:], tanh[:], 0.5, 0.5, ALU.mult, ALU.add).then_inc(s_tanh2, 1)
                dve.wait_ge(s_tanh2, n + 1)
                nc.vector.tensor_tensor(cw[:, 0:E * TG].rearrange("p (e g) -> p g e", e=E), tanh[:], wins[:],
                                        ALU.mult).then_inc(s_cw, 1)

            def gate_turned(n):
                dve.wait_ge(s_cwp, n + 1)
                nc.vector.tensor_copy(cw_t[:], ps[0:E * TG, 7, 0:P]).then_inc(s_cwt, 1)

            def hidden_low(m, c):
                dve.wait_ge(s_hi, m + 1)
                nc.vector.tensor_tensor(hid_lo[:, c % RING], hid[:, c % 2], hid_hi[:, c % RING].bitcast(F32),
                                        ALU.subtract).then_inc(s_lo, 1)

            def weigh(r, k):
                t, e, y = k // STEPS, k % STEPS // FC, 8 * r + k // FC
                dve.wait_ge(s_y, y + 1)
                dve.wait_ge(s_cwb, 2 * r + t + 1)
                dve.wait_ge(s_acc, y + 1)
                for h in range(2):
                    nc.vector.scalar_tensor_tensor(
                        y_w[:, (k // FC) % 2, h * HALF:(h + 1) * HALF], ps_y[:, h], b2s[:, e:e + 1],
                        cw_all[:, t, e, h * HALF:(h + 1) * HALF], ALU.add, ALU.mult).then_inc(s_stt, 1)

            def finish(n):
                dve.wait_ge(s_ftp, n + 1)
                nc.vector.tensor_tensor(xb[:, 4 * n:4 * n + 4], ps[:, 6 + n % 2].rearrange("p (b d) -> p b d", d=D),
                                        x1[:, 4 * n:4 * n + 4], ALU.add).then_inc(s_fin, 1)

            def round_(r, last):
                for k in range(RS):
                    for t, n, rn, k0 in ((1, 2 * r + 1, r, 0), (0, 2 * r + 2, r + 1, STEPS)):
                        if k0 and last:
                            continue
                        if k == k0 + 7:
                            gate_logits(n, rn)
                        if k == k0 + 8:
                            gate_top2(n)
                        if k == k0 + 9:
                            gate_args(n)
                        if k == k0 + 10:
                            gate_beats(n)
                        if k == k0 + 11:
                            gate_wins(n)
                        if k == k0 + 12:
                            gate_weights(n)
                        if k == k0 + 13:
                            gate_turned(n)
                    if k % FC == FC - 1:
                        weigh(r, k)
                    if last and k == STEPS + 4:
                        finish(0)
                        finish(1)
                    if k + LAG - 1 < RS or not last:
                        hidden_low(RS * r + k + LAG - 1, (k + LAG - 1) % STEPS)

            gate_logits(0, 0)
            normalise_x1(3)
            gate_top2(0)
            gate_args(0)
            gate_beats(0)
            gate_wins(0)
            hidden_low(0, 0)
            gate_weights(0)
            cur_low(2)
            cur_low(3)
            dve.wait_ge(s_cur3, NQ)
            dve.sem_inc(s_stt, 2)
            gate_turned(0)
            hidden_low(1, 1)
            with dve.Fori(0, R - 1) as r:
                round_(r, False)
            round_(R - 1, True)
            finish(2)
            finish(3)

        @block.tensor
        def _(pe):
            def product(dst, w_hi, w_lo, a_hi, a_lo, start=True, stop=True):
                nc.tensor.matmul(dst, w_hi, a_lo, start=start, stop=False)
                nc.tensor.matmul(dst, w_lo, a_hi, start=False, stop=False)
                return nc.tensor.matmul(dst, w_hi, a_hi, start=False, stop=stop)

            pe.wait_ge(s_ident, 1)
            pe.wait_ge(s_wsplit, 2)
            def keys_and_values(q):
                quad = slice(q * QK, (q + 1) * QK)
                pe.wait_ge(s_ctx, q + 1)
                if q >= 2:
                    pe.wait_ge(s_kf, q - 1)
                    pe.wait_ge(s_vf, q - 1)
                product(ps[:, 2 + q % 2, 0:QK], wqkv_hi[:, 1], wqkv_lo[:, 1], ctx_hi[:, quad], ctx_lo[:, quad])\
                    .then_inc(s_kp, 1)
                for b in range(QUAD):
                    keys = slice((q * QUAD + b) * KEYS, (q * QUAD + b + 1) * KEYS)
                    last = product(ps[0:KEYS, 4 + q % 2, b * D:(b + 1) * D], ctx_hi[:, keys], ctx_lo[:, keys],
                                   wqkv_hi[:, 2], wqkv_lo[:, 2])
                last.then_inc(s_vp, 1)

            def turn_tokens(q):
                pe.wait_ge(s_xn, q + 1)
                if q >= 2:
                    pe.wait_ge(s_xtl, q - 1)
                for b in range(QUAD):
                    last = nc.tensor.transpose(ps[:, q % 2, b * S:(b + 1) * S], xn[:, q % 2, b], ident[:])
                last.then_inc(s_xtp, 1)

            def queries(q):
                pe.wait_ge(s_xtl, q + 1)
                if q >= 2:
                    pe.wait_ge(s_qf, q - 1)
                product(ps[:, 6 + q % 2], wqkv_hi[:, 0], wqkv_lo[:, 0], xt_hi[:, q % 2], xt_lo[:, q % 2]).then_inc(s_qp, 1)

            keys_and_values(0)
            keys_and_values(1)
            for i in range(NQ + 1):
                if i < NQ:
                    turn_tokens(i)
                if i >= 1:
                    queries(i - 1)
                if i + 2 < NQ:
                    keys_and_values(i + 2)

            def scores(u, b, half, slot):
                if half == 0:
                    pe.wait_ge(s_q_slot, b + 1)
                    pe.wait_ge(s_k_slot, 2 * b + 2)
                if not (isinstance(u, int) and u < 2):
                    pe.wait_ge(s_exp, u - 1)
                rows = slice(64 * half, 64 * half + 64)
                for step, (qp, kp) in enumerate(((0, 1), (1, 0), (0, 0))):
                    for g in range(2):
                        last = nc.tensor.matmul(ps_score[:, 2 * half + g, 0:J * KEYS], q_slot[rows, slot, qp],
                                                k_slot[slot][rows, kp, g].rearrange("p j k -> p (j k)"),
                                                start=(step == 0), stop=(step == 2))
                last.then_inc(s_score, 1)

            def turn_probs(u, half):
                pe.wait_ge(s_exp, u + 1)
                for bank in range(2):
                    if not (isinstance(u, int) and u < 1):
                        pe.wait_ge(s_pt, 2 * u + bank - 1)
                    for i in range(HH // 2):
                        last = nc.tensor.transpose(ps_pt[:, bank, i], probs[:, half, bank * HH // 2 + i], ident[:])
                    last.then_inc(s_ptp, 1)

            def values(u, b, half, slot):
                pe.wait_ge(s_pt, 2 * u + 2)
                if half == 0:
                    pe.wait_ge(s_v_slot, b + 1)
                    if not (isinstance(b, int) and b < 2):
                        pe.wait_ge(s_attn, b - 1)
                for i in range(HH):
                    h, bank = half * HH + i, i // (HH // 2)
                    for part in range(2):
                        last = nc.tensor.matmul(ps_o[:, slot, h].rearrange("p c d -> p (c d)"),
                                                probs_t[:, half, part, bank, i % (HH // 2)],
                                                v_slot[:, slot, h * 3 * (DH + 1):(h + 1) * 3 * (DH + 1)],
                                                start=(part == 0), stop=(part == 1))
                last.then_inc(s_pv, 1)

            def turn_attn(q):
                pe.wait_ge(s_attn, (q + 1) * QUAD)
                if q >= 2:
                    pe.wait_ge(s_at, q - 1)
                else:
                    pe.wait_ge(s_exp, 2 * NB - 1)
                for b in range(QUAD):
                    last = nc.tensor.transpose(ps[:, q % 2, b * S:(b + 1) * S], attn[:, q * QUAD + b], ident[:])
                last.then_inc(s_atp, 1)

            def project(q):
                pe.wait_ge(s_at, q + 1)
                if q >= 2:
                    pe.wait_ge(s_x1, q - 1)
                else:
                    pe.wait_ge(s_exp, 2 * NB)
                    pe.wait_ge(s_in_o, 32)
                for b in range(QUAD):
                    last = nc.tensor.matmul(ps[:, 2 + q % 2, b * D:(b + 1) * D], attn_t[:, q % 2, b * S:(b + 1) * S],
                                            wo[:], start=True, stop=True)
                last.then_inc(s_op, 1)

            def pair(p, last):
                for n in range(4):
                    u = 4 * p + n
                    if not (last and n >= 1):
                        scores(u + 3, 2 * p + (n + 3) // 2, (n + 3) % 2, (n + 3) // 2 % 2)
                    if not (last and n == 3):
                        turn_probs(u + 1, (n + 1) % 2)
                    if last and n == 1:
                        turn_attn(0)
                        turn_attn(1)
                    values(u, 2 * p + n // 2, n % 2, n // 2)
                    if last and n >= 2:
                        project(n - 2)

            pe.wait_ge(s_kf, NQ)
            pe.wait_ge(s_qf, NQ)
            pe.wait_ge(s_vf, NQ)
            scores(0, 0, 0, 0)
            scores(1, 0, 1, 0)
            scores(2, 1, 0, 1)
            turn_probs(0, 0)
            pair(0, False)
            with pe.Fori(1, NB // 2 - 1) as p:
                pair(p, False)
            pair(NB // 2 - 1, True)

            def turn_cur(q):
                pe.wait_ge(s_xn, NQ + q + 1)
                for b in range(QUAD):
                    last = nc.tensor.transpose(ps_ct[q][:, b * S:(b + 1) * S], xn[:, q % 2, b], ident[:])
                last.then_inc(s_ctp, 1)

            turn_attn(2)
            project(2)
            turn_attn(3)
            project(3)
            turn_cur(0)
            turn_cur(1)

            def gate(t, n, r):
                if isinstance(n, int) and n == 0:
                    pe.wait_ge(s_ct, 2 * (NQ // 2))
                    pe.wait_ge(s_cur3, 1)
                else:
                    pe.wait_ge(s_split, n + 1)
                for i in range(TG):
                    last = nc.tensor.matmul(ps[:, 6, i * E:(i + 1) * E], cur[:, t, i * P:(i + 1) * P],
                                            wgs[:, bass.ds(r * E, E)], start=True, stop=True)
                last.then_inc(s_gl, 1)

            def turn_gate(n):
                pe.wait_ge(s_cw, n + 1)
                nc.tensor.transpose(ps[:, 7, 0:P], cw[:], ident[:]).then_inc(s_cwp, 1)

            def first(m, c, t, n, wait_slot=True):
                if c == 0:
                    pe.wait_ge(s_split, n + 1)
                if wait_slot:
                    pe.wait_ge(s_gelu, m - 1)
                w = slice(c * P, (c + 1) * P)
                for h in range(2):
                    cols = slice(h * HALF, (h + 1) * HALF)
                    last = product(ps_h[:, c % 2, cols], w1_hi[:, w], w1_lo[:, w], cur_hi[:, t, cols], cur_lo[:, t, cols])
                last.then_inc(s_w1, 1)

            def second(r, k):
                c, y = k % STEPS, 8 * r + k // FC
                pe.wait_ge(s_lo, RS * r + k + 1)
                w = slice(c * P, (c + 1) * P)
                for h in range(2):
                    if c % FC == 0:
                        pe.wait_ge(s_stt, 2 * y + h + 1)
                    cols = slice(h * HALF, (h + 1) * HALF)
                    last = product(ps_y[:, h], w2_hi[:, w], w2_lo[:, w], hid_hi[:, c % RING, cols],
                                   hid_lo[:, c % RING, cols], c % FC == 0, c % FC == FC - 1)
                if c % FC == FC - 1:
                    last.then_inc(s_y, 1)

            def turn_back(n):
                t = n // 2
                pe.wait_ge(s_acc, 8 * (R - 1) + 4 * t + 6)
                for i in range(4):
                    c = (n % 2) * 4 + i
                    last = nc.tensor.transpose(ps[:, 6 + n % 2, i * P:(i + 1) * P], cur[:, t, c * P:(c + 1) * P], ident[:])
                last.then_inc(s_ftp, 1)

            def round_(r, last):
                for k in range(RS):
                    if k == 6:
                        gate(1, 2 * r + 1, r)
                    if k == 22 and not last:
                        gate(0, 2 * r + 2, r + 1)
                    if k == 13:
                        turn_gate(2 * r + 1)
                    if k == 29 and not last:
                        turn_gate(2 * r + 2)
                    if last and k == STEPS + 3:
                        turn_back(0)
                        turn_back(1)
                    second(r, k)
                    a = k + LAG
                    if a < RS:
                        first(RS * r + a, a % STEPS, a // STEPS, 2 * r + a // STEPS)
                    elif not last:
                        first(RS * r + a, a % STEPS, 0, 2 * r + 2)

            gate(0, 0, 0)
            pe.wait_ge(s_fsplit, 2)
            first(0, 0, 0, 0, wait_slot=False)
            turn_cur(2)
            turn_cur(3)
            first(1, 1, 0, 0, wait_slot=False)
            first(2, 2, 0, 0)
            turn_gate(0)
            with pe.Fori(0, R - 1) as r:
                round_(r, False)
            round_(R - 1, True)
            turn_back(2)
            turn_back(3)


def kernel(x, ctx_1024, L0_xattn_wq, L0_xattn_bq, L0_xattn_wk, L0_xattn_bk, L0_xattn_wv, L0_xattn_bv, L0_xattn_wo,
           L0_xattn_bo, L0_ffn_Wg, L0_ffn_bg, L0_ffn_W1, L0_ffn_b1, L0_ffn_W2, L0_ffn_b2):
    import numpy as np
    import concourse.bacc as bacc
    from concourse.bass_utils import run_bass_kernel_spmd

    def laid(a):
        return np.ascontiguousarray(a)

    D = x.shape[-1]
    ctx = np.asarray(ctx_1024)
    arrays = {
        "x": laid(x),
        "ctx_t": laid(ctx.reshape(-1, D).T),
        "w_qkv": laid(np.stack([np.asarray(w).T for w in (L0_xattn_wq, L0_xattn_wk, L0_xattn_wv)], axis=1)),
        "w_o": laid(np.asarray(L0_xattn_wo).T),
        "b_qk": laid(np.stack([np.asarray(L0_xattn_bq), np.asarray(L0_xattn_bk)], axis=1)),
        "b_v": laid(L0_xattn_bv),
        "b_o": laid(L0_xattn_bo),
        "wg": laid(np.asarray(L0_ffn_Wg).transpose(1, 0, 2).reshape(D, -1)),
        "bg": laid(np.asarray(L0_ffn_bg).reshape(-1)),
        "w1": laid(L0_ffn_W1),
        "b1": laid(np.asarray(L0_ffn_b1).reshape(-1, 128).T),
        "w2": laid(np.asarray(L0_ffn_W2).reshape(-1, D)),
        "b2": laid(np.asarray(L0_ffn_b2).T),
    }
    nc = bacc.Bacc("TRN2", target_bir_lowering=False, num_devices=1)
    args = [nc.dram_tensor(f"in_{name}", a.shape, mybir.dt.from_np(a.dtype), kind="ExternalInput").ap()
            for name, a in arrays.items()]
    out = nc.dram_tensor("out_0", arrays["x"].shape, F32, kind="ExternalOutput").ap()
    xattn_moe(nc, *args, out)
    r = run_bass_kernel_spmd(nc, [{f"in_{name}": a for name, a in arrays.items()}], core_ids=[0])
    return r.results[0]["out_0"]
```
